# Optimizing a Trainium2 kernel written in Bass

```python
import numpy as np
import jax
import jax.numpy as jnp

def _softmax(x, axis=-1):
    return jax.nn.softmax(x, axis=axis)

def _gelu(x):
    return jax.nn.gelu(x, approximate=True)

def _silu(x):
    return jax.nn.silu(x)

def _sigmoid(x):
    return jax.nn.sigmoid(x)

def _layernorm(x, axis=-1, eps=1e-05):
    m = jnp.mean(x, axis=axis, keepdims=True)
    v = jnp.var(x, axis=axis, keepdims=True)
    return (x - m) / jnp.sqrt(v + eps)

def _scatter_add(tgt, idx, src, axis=0):
    return tgt.at[idx].add(src)

def _segment_sum(src, seg, n):
    return jax.ops.segment_sum(src, seg, n)
kernel_name = 'mk_adj_preln_d4_adj_r2_fd851d'

def setup_inputs(seed: int=0):
    np.random.seed(seed)
    _w = jnp.asarray

    def _rec_inputs():
        import jax
        import jax.numpy as jnp
        _gk = jax.random.key(seed)
        x = -0.000929 + 1 * jax.random.normal(jax.random.fold_in(_gk, 1), (8, 1024, 64), jnp.float32)
        _w = (1.0 + jnp.arange(1024, dtype=jnp.float32)) ** (-0.5)
        _w = _w / _w.mean()
        _pij = jnp.clip(0.00195312 * _w[:, None] * _w[None, :], 0.0, 1.0)
        _a = jax.random.uniform(jax.random.fold_in(_gk, 2), (1024, 1024)) < _pij
        adj = _a.astype(jnp.int32)
        return (x, adj)
    x, adj = _rec_inputs()

    def _L0_gnn_setup():
        import jax, jax.numpy as jnp
        import numpy as np
        ALPHA = 0.2
        NEG_INF = -9000000000000000.0
        key = jax.random.key(seed)
        k1, k2, k3, k4 = jax.random.split(key, 4)
        B, N, Fin, Fout = (8, 1024, 64, 64)
        inp = jax.random.normal(k1, (B, N, Fin), dtype=jnp.float32)
        adj = jax.random.randint(k2, (N, N), 0, 2, dtype=jnp.int32)
        W = jax.random.normal(k3, (Fin, Fout), dtype=jnp.float32) * np.sqrt(2.0 / Fout)
        a = jax.random.normal(k4, (2 * Fout, 1), dtype=jnp.float32) * np.sqrt(2.0 / (2 * Fout + 1))
        return {'input': inp, 'adj': adj, 'W': W, 'a': a}
    _L0_gnn_all = _L0_gnn_setup()
    _L0_gnn_in = {k: v for k, v in _L0_gnn_all.items() if k in ('W', 'a')}
    del _L0_gnn_all

    def _L1_gnn_setup():
        import jax, jax.numpy as jnp
        import numpy as np
        B, N, F_IN, F_OUT = (8, 4096, 64, 64)
        LN_EPS = 1e-05
        key = jax.random.key(seed)
        k_x, k_adj, k_ws, k_wn = jax.random.split(key, 4)
        scale = 1.0 / np.sqrt(F_IN)
        return {'x': jax.random.normal(k_x, (B, N, F_IN), dtype=jnp.float32), 'adj_matrix': jax.random.randint(k_adj, (N, N), 0, 2, dtype=jnp.int32), 'W_self': jax.random.normal(k_ws, (F_IN, F_OUT), dtype=jnp.float32) * scale, 'b_self': jnp.zeros((F_OUT,), dtype=jnp.float32), 'W_neigh': jax.random.normal(k_wn, (F_IN, F_OUT), dtype=jnp.float32) * scale, 'b_neigh': jnp.zeros((F_OUT,), dtype=jnp.float32), 'ln_gamma': jnp.ones((F_OUT,), dtype=jnp.float32), 'ln_beta': jnp.zeros((F_OUT,), dtype=jnp.float32)}
    _L1_gnn_all = _L1_gnn_setup()
    _L1_gnn_in = {k: v for k, v in _L1_gnn_all.items() if k in ('W_self', 'b_self', 'W_neigh', 'b_neigh', 'ln_gamma', 'ln_beta')}
    del _L1_gnn_all

    def _L2_gnn_setup():
        import jax, jax.numpy as jnp
        import numpy as np
        INV_SQRT2 = 0.7071067811865476
        key = jax.random.key(seed)
        k = jax.random.split(key, 6)
        batch, node, dim = (4, 256, 64)
        x = jax.random.normal(k[0], (batch, node, dim), dtype=jnp.float32)
        w0 = jax.random.normal(k[1], (1, 1), dtype=jnp.float32)
        b0 = jax.random.normal(k[2], (1,), dtype=jnp.float32)
        wa = jax.random.normal(k[3], (dim,), dtype=jnp.float32)
        ba = jax.random.normal(k[4], (dim,), dtype=jnp.float32)
        adj = jax.random.randint(k[5], (node, node), 0, 2, dtype=jnp.int32)
        return {'x': x, 'w0': w0, 'b0': b0, 'wa': wa, 'ba': ba, 'adj': adj}
    _L2_gnn_all = _L2_gnn_setup()
    _L2_gnn_in = {k: v for k, v in _L2_gnn_all.items() if k in ('w0', 'b0', 'wa', 'ba')}
    del _L2_gnn_all

    def _L3_gnn_setup():
        import jax, jax.numpy as jnp
        import numpy as np
        ALPHA = 0.2
        MASK_VAL = -9000000000000000.0
        B, N, FIN, FOUT = (8, 1024, 64, 64)
        key = jax.random.key(seed)
        k1, k2, k3, k4 = jax.random.split(key, 4)
        x = jax.random.normal(k1, (B, N, FIN), dtype=jnp.float32)
        adj = jax.random.randint(k2, (N, N), 0, 2, dtype=jnp.int32)
        W = jax.random.normal(k3, (FOUT, FIN), dtype=jnp.float32) * 0.1
        a = jax.random.normal(k4, (2 * FOUT, 1), dtype=jnp.float32) * 0.1
        return {'x': x, 'adj': adj, 'W': W, 'a': a}
    _L3_gnn_all = _L3_gnn_setup()
    _L3_gnn_in = {k: v for k, v in _L3_gnn_all.items() if k in ('W', 'a')}
    del _L3_gnn_all
    return {'x': x, 'adj': adj, 'L0_gnn_W': _L0_gnn_in['W'], 'L0_gnn_a': _L0_gnn_in['a'], 'L1_gnn_W_self': _L1_gnn_in['W_self'], 'L1_gnn_b_self': _L1_gnn_in['b_self'], 'L1_gnn_W_neigh': _L1_gnn_in['W_neigh'], 'L1_gnn_b_neigh': _L1_gnn_in['b_neigh'], 'L1_gnn_ln_gamma': _L1_gnn_in['ln_gamma'], 'L1_gnn_ln_beta': _L1_gnn_in['ln_beta'], 'L2_gnn_w0': _L2_gnn_in['w0'], 'L2_gnn_b0': _L2_gnn_in['b0'], 'L2_gnn_wa': _L2_gnn_in['wa'], 'L2_gnn_ba': _L2_gnn_in['ba'], 'L3_gnn_W': _L3_gnn_in['W'], 'L3_gnn_a': _L3_gnn_in['a']}

def reference(x, adj, L0_gnn_W, L0_gnn_a, L1_gnn_W_self, L1_gnn_b_self, L1_gnn_W_neigh, L1_gnn_b_neigh, L1_gnn_ln_gamma, L1_gnn_ln_beta, L2_gnn_w0, L2_gnn_b0, L2_gnn_wa, L2_gnn_ba, L3_gnn_W, L3_gnn_a):
    import jax
    import jax.numpy as jnp

    def _L0_gnn_ref(input, adj, W, a):
        import jax, jax.numpy as jnp
        import numpy as np
        ALPHA = 0.2
        NEG_INF = -9000000000000000.0
        h = jnp.matmul(input, W)
        Fout = W.shape[1]
        a1 = a[:Fout, 0]
        a2 = a[Fout:, 0]
        s1 = jnp.einsum('bnf,f->bn', h, a1)
        s2 = jnp.einsum('bnf,f->bn', h, a2)
        e = s1[:, :, None] + s2[:, None, :]
        e = jnp.where(e > 0, e, ALPHA * e)
        masked = jnp.where(adj[None, :, :] > 0, e, NEG_INF)
        attention = jax.nn.softmax(masked, axis=-1)
        h_prime = jnp.matmul(attention, h)
        return jax.nn.elu(h_prime)

    def _L1_gnn_ref(x, adj_matrix, W_self, b_self, W_neigh, b_neigh, ln_gamma, ln_beta):
        import jax, jax.numpy as jnp
        import numpy as np
        B, N, F_IN, F_OUT = (8, 4096, 64, 64)
        LN_EPS = 1e-05
        A = (adj_matrix > 0).astype(x.dtype)
        deg = A.sum(axis=1)
        agg = jnp.einsum('ij,bjf->bif', A, x)
        agg = agg / jnp.maximum(deg, 1.0)[None, :, None]
        neigh_out = agg @ W_neigh + b_neigh
        neigh_out = jnp.where((deg > 0)[None, :, None], neigh_out, 0.0)
        self_out = x @ W_self + b_self
        out = jax.nn.relu(self_out + neigh_out)
        out = jax.nn.relu(out)
        mu = out.mean(axis=-1, keepdims=True)
        var = jnp.mean((out - mu) ** 2, axis=-1, keepdims=True)
        out = (out - mu) * jax.lax.rsqrt(var + LN_EPS) * ln_gamma + ln_beta
        return out

    def _L2_gnn_ref(x, w0, b0, wa, ba, adj):
        import jax, jax.numpy as jnp
        import numpy as np
        INV_SQRT2 = 0.7071067811865476
        feat = jax.nn.softplus(x * (INV_SQRT2 * w0[0, 0]) + b0[0])
        scores = feat * wa + ba
        mask = adj > 0
        logits = scores[:, None, :, :] * mask[None, :, :, None].astype(scores.dtype)
        logits = jnp.where(mask[None, :, :, None], logits, jnp.float32(-1000000000.0))
        attn = jax.nn.softmax(logits, axis=2)
        out = jnp.einsum('bijd,bjd->bid', attn, feat)
        return out

    def _L3_gnn_ref(x, adj, W, a):
        import jax, jax.numpy as jnp
        import numpy as np
        ALPHA = 0.2
        MASK_VAL = -9000000000000000.0
        B, N, FIN, FOUT = (8, 1024, 64, 64)
        h = jnp.einsum('bnf,of->bno', x, W)
        f_out = h.shape[-1]
        a1 = a[:f_out, 0]
        a2 = a[f_out:, 0]
        e_i = h @ a1
        e_j = h @ a2
        e = jax.nn.leaky_relu(e_i[:, :, None] + e_j[:, None, :], negative_slope=ALPHA)
        e = jnp.where(adj[None, :, :] > 0, e, MASK_VAL)
        attention = jax.nn.softmax(e, axis=2)
        h_prime = jnp.einsum('bij,bjo->bio', attention, h)
        return jax.nn.relu(h_prime)
    h = jnp.maximum(_layernorm(x, axis=-1), 0.0)
    x = x + _L0_gnn_ref(h, adj, L0_gnn_W, L0_gnn_a)
    h = jnp.maximum(_layernorm(x, axis=-1), 0.0)
    x = x + _L1_gnn_ref(h, adj, L1_gnn_W_self, L1_gnn_b_self, L1_gnn_W_neigh, L1_gnn_b_neigh, L1_gnn_ln_gamma, L1_gnn_ln_beta)
    h = jnp.maximum(_layernorm(x, axis=-1), 0.0)
    x = x + _L2_gnn_ref(h, L2_gnn_w0, L2_gnn_b0, L2_gnn_wa, L2_gnn_ba, adj)
    h = jnp.maximum(_layernorm(x, axis=-1), 0.0)
    x = x + _L3_gnn_ref(h, adj, L3_gnn_W, L3_gnn_a)
    return x

_drawn_inputs = setup_inputs


def setup_inputs(seed=0):
    import zlib

    import numpy as np

    out = dict(_drawn_inputs(seed))
    spreads = {'L1_gnn_b_self': (0.0, 0.1),
     'L1_gnn_b_neigh': (0.0, 0.1),
     'L1_gnn_ln_gamma': (1.0, 0.2),
     'L1_gnn_ln_beta': (0.0, 0.1)}
    factors = {'L2_gnn_ba': 8.0, 'L3_gnn_a': 4.133}
    for name, (base, spread) in spreads.items():
        noise = np.random.default_rng([zlib.crc32(name.encode()), seed]).standard_normal(out[name].shape)
        drawn = base * np.exp(spread * noise) if base else spread * noise
        out[name] = jnp.asarray(drawn.astype(out[name].dtype))
    for name, factor in factors.items():
        out[name] = (out[name] * factor).astype(out[name].dtype)
    return out
```

```python
from contextlib import ExitStack

import concourse.bass as bass
from concourse import mybir

ALU = mybir.AluOpType
ACT = mybir.ActivationFunctionType
F32 = mybir.dt.float32
BF16 = mybir.dt.bfloat16
I32 = mybir.dt.int32
AX_X = mybir.AxisListType.X


P = 128
ATT0, MEAN, CHAN, ATT3 = range(4)
LAYERS = 4
EPS = 1e-5
SLOPE = 0.2
BIG = float(2.0 ** 100)
BIG_E = float(2.0 ** 80)


def build(nc, x_in, adj_in, w_in, out):
    B, N, D = x_in.shape
    T = N // P
    G = D + 2
    V = D + 1
    VQ = 2 * V
    CH = T // 2
    NR = 6

    with ExitStack() as ctx:
        def sb(name, shape, dt=F32):
            return ctx.enter_context(nc.sbuf_tensor(name, shape, dt))

        def ps(name, shape):
            return ctx.enter_context(nc.psum_tensor(name, shape, F32))

        def sem(name):
            return ctx.enter_context(nc.semaphore(name))

        x = sb("x", [P, B, T, D])
        maskT = sb("maskT", [P, T, N], BF16)
        nmaskT = sb("nmaskT", [P, T, N], BF16)
        deg = sb("deg", [P, T])
        deg1 = sb("deg1", [P, T])
        rdeg = sb("rdeg", [P, T])
        lone = sb("lone", [P, T])
        some = sb("some", [P, T])
        base = sb("base", [P, T, D])
        ones = sb("ones", [P, P])
        ident = sb("ident", [P, P])
        identb = sb("identb", [P, P], BF16)
        avg = sb("avg", [P, P])
        mhalf = sb("mhalf", [P, T])
        rows = sb("rows", [1, NR * D + 2])
        par_rows = sb("par_rows", [P, NR * D + 2])
        k0 = sb("k0", [P, 1])
        b0 = sb("b0", [P, 1])
        wnat = [sb(f"wnat{g}", [D, D]) for g in range(2)]
        wtr = [sb(f"wtr{g}", [D, D]) for g in range(2)]
        acol = [sb(f"acol{g}", [D, 2]) for g in range(2)]
        arep = [sb(f"arep{g}", [D, P]) for g in range(2)]
        wext = [sb(f"wext{g}", [P, G]) for g in range(2)]
        w1rep = [sb(f"w1rep{g}", [P, P]) for g in range(2)]
        wconv = sb("wconv", [P, 2 * D])
        mean = sb("mean", [P, T])
        cent = sb("cent", [P, T, D])
        sq = sb("sq", [P, T, D])
        var = sb("var", [P, T])
        vare = sb("vare", [P, T])
        rstd = sb("rstd", [P, T])
        h = sb("h", [P, 2, T, D])
        hT = sb("hT", [P, T // 2, P])
        hp = sb("hp", [P, 2, T, G + 2])
        s1bc = sb("s1bc", [P, N])
        hc = sb("hc", [P, 2, T, 2 * D])
        selfp = sb("selfp", [P, 2, T, D])
        smx = sb("smx", [P, P])
        mcol = sb("mcol", [D, 1])
        mdiag = sb("mdiag", [D, D])
        s2big = sb("s2big", [P, 2, T])
        z08 = sb("z08", [P, T])
        pre = sb("pre", [P, 4, T])
        ex = sb("ex", [P, 2, 4, T])
        vq = sb("vq", [P, 2, 2, T])
        reach = sb("reach", [P, T, N], BF16)
        C = sb("C", [P, 2, T, N], BF16)
        adj = C[:].rearrange("p a t n -> p (a t n)").bitcast(I32).rearrange("p (t n) -> p t n", t=T)
        mask = reach
        top = sb("top", [P, 2, T, VQ])
        rest = sb("rest", [P, 2, T, VQ])
        low = sb("low", [P, 2, T, VQ], BF16)
        ab = sb("ab", [P, T, D])
        sp = sb("sp", [P, T, D])
        rl = sb("rl", [P, T, D])
        feat = sb("feat", [P, 2, T, D])
        sc = sb("sc", [P, T, D])
        ee = sb("ee", [P, T, D])
        hm = sb("hm", [P, D])
        num = sb("num", [P, T, VQ])
        tq = sb("tq", [P, T, V])
        rden = sb("rden", [P, T, D])
        att = sb("att", [P, T, D])
        lz = sb("lz", [P, T, D])
        neg = sb("neg", [P, T, D])
        en = sb("en", [P, T, D])
        so = sb("so", [P, T, D])
        osum = sb("osum", [P, T])
        ovar = sb("ovar", [P, T])
        ovare = sb("ovare", [P, T])
        orstd = sb("orstd", [P, T])
        oc = sb("oc", [P, T, D])
        osq = sb("osq", [P, T, D])

        acc = ps("acc", [P, CH, 512])
        tp = ps("tp", [P, 2, 512])
        pj = ps("pj", [P, 2, 512])

        names = """adj_in x_in0 x_in1 x_in2 w_in const_g ident_g identb_g rows_ps rows_sb wt_ps wt_sb arep_sb wa_ps wa_sb
            mask_nat mask_tr acc_free nmask_sb deg_sb lone_sb deg1_sb rdeg_sb some_sb base_sb base2_sb scal_sb hp_one
            ln_sum ln_mean ln_cent ln_sq ln_ss ln_var ln_rstd h_done tr_done hT_done pj_done mxt_done mcol_done mdiag_done mbc_done s1_done hp_done s1bc_done hc_done self_done
            smx_done s2big_done z08_done pre_done ex_done vq_done reach_done c_done top_done rest_done low_done
            ab_done e1_done ln1_done rl_done feat_done sc1_done sc_done scm_done ee_done chE_done
            avg_done hm_done main_done  num_done den_done rden_done att1 lz_done att_done neg_done en_done so_done
            g1 g2 g3 g4 g5 g6 g7 g8 g9 g10 g11 x_done out_done""".split()
        S = {n: sem(n) for n in names}

        def item(l, b):
            return B * l + b + 1

        def att_item(l, b):
            return B * (l // 3) + b + 1

        def avg_item(l, b):
            return B * (0, 0, 1, 2)[l] + b + 1

        def tr_item(l, b):
            return B * (0, 1, 1, 2)[l] + b + 1

        def freed(l, b, c):
            return T + CH * (item(l, b) - 1) + c

        def upper(t):
            return t.bitcast(BF16).rearrange("p t (v two) -> p t v two", two=2)[:, :, :, 1]

        def spread(t, d):
            return t.unsqueeze(2).to_broadcast([P, t.shape[1], d])

        def along(r):
            return r.unsqueeze(1).to_broadcast([P, T, r.shape[1]])

        width = (VQ, D, 2 * D, VQ)

        def par_row(n):
            return par_rows[:, n * D:(n + 1) * D]

        B_SELF, B_NEIGH, GAMMA, BETA, WA, BA = range(NR)

        def walk(eng, step):
            for l in range(LAYERS):
                with eng.Fori(0, B - 3, 2) as b:
                    step((l, b + 2), (l, b + 1), (l, b), 0)
                    step((l, b + 3), (l, b + 2), (l, b + 1), 1)
                more = l + 1 < LAYERS
                step((l + 1, 0) if more else None, (l, B - 1), (l, B - 2), 0)
                step((l + 1, 1) if more else None, (l + 1, 0) if more else None, (l, B - 1), 1)

        block = ctx.enter_context(nc.Block())

        @block.sync
        def _(sync):
            xv = x_in.rearrange("b (p t) d -> p b (t d)", t=T)
            xs = x[:].rearrange("p b t d -> p b (t d)")
            av = adj_in.rearrange("(p t) n -> p t n", t=T)
            sync.dma_start(xs[:, 0:1], xv[:, 0:1]).then_inc(S["x_in0"], 16)
            for g, (w, a) in enumerate(((w_in["L0_gnn_W"], w_in["L0_gnn_a"]), (w_in["L3_gnn_W"], w_in["L3_gnn_a"]))):
                sync.dma_start(wnat[g][:], w).then_inc(S["w_in"], 16)
                for c in range(2):
                    sync.dma_start(acol[g][:, c:c + 1], a[c * D:(c + 1) * D, :]).then_inc(S["w_in"], 16)
            for half in range(2):
                sync.dma_start(wconv[half * D:half * D + D, 0:D], w_in["L1_gnn_W_self"]).then_inc(S["w_in"], 16)
                sync.dma_start(wconv[half * D:half * D + D, D:2 * D], w_in["L1_gnn_W_neigh"]).then_inc(S["w_in"], 16)
            for n, name in enumerate(("L1_gnn_b_self", "L1_gnn_b_neigh", "L1_gnn_ln_gamma", "L1_gnn_ln_beta",
                                      "L2_gnn_wa", "L2_gnn_ba")):
                sync.dma_start(rows[0:1, n * D:(n + 1) * D], w_in[name].rearrange("(o d) -> o d", o=1)).then_inc(S["w_in"], 16)
            sync.dma_start(rows[0:1, NR * D:NR * D + 1], w_in["L2_gnn_w0"]).then_inc(S["w_in"], 16)
            sync.dma_start(rows[0:1, NR * D + 1:NR * D + 2],
                           w_in["L2_gnn_b0"].rearrange("(o d) -> o d", o=1)).then_inc(S["w_in"], 16)
            sync.dma_start(xs[:, 1:2], xv[:, 1:2]).then_inc(S["x_in1"], 16)
            sync.dma_start(adj, av).then_inc(S["adj_in"], 16)
            sync.dma_start(xs[:, 2:B], xv[:, 2:B]).then_inc(S["x_in2"], 16)
            ov = out.rearrange("b (p t) d -> p b (t d)", t=T)
            for b in range(B):
                sync.wait_ge(S["x_done"], item(ATT3, b))
                sync.dma_start(ov[:, b:b + 1], xs[:, b:b + 1]).then_inc(S["out_done"], 16)
            sync.wait_ge(S["out_done"], 16 * B)
        W_IN = 16 * 18

        @block.gpsimd
        def _(pool):
            nc.gpsimd.memset(ones[:], 1.0)
            nc.gpsimd.memset(avg[:], 1.0 / N)
            nc.gpsimd.memset(mhalf[:], -0.5)
            nc.gpsimd.memset(smx[:], 0.0)
            nc.gpsimd.memset(hp[:, :, :, G:G + 1], 1.0)
            nc.gpsimd.memset(ident[:], 0.0).then_inc(S["const_g"], 1)
            pool.wait_ge(S["const_g"], 1)
            nc.gpsimd.affine_select(out=ident[:], in_=ident[:], compare_op=ALU.not_equal, fill=1.0, base=0,
                                    pattern=[[-1, P]], channel_multiplier=1).then_inc(S["ident_g"], 1)
            pool.wait_ge(S["ident_g"], 1)
            nc.gpsimd.tensor_copy(identb[:], ident[:]).then_inc(S["identb_g"], 1)

            def rstd_A(l, b):
                pool.wait_ge(S["ln_var"], item(l, b))
                nc.gpsimd.tensor_tensor(rstd[:], vare[:], mhalf[:], ALU.pow).then_inc(S["ln_rstd"], 1)

            def rstd_M(l, b):
                if l == MEAN:
                    pool.wait_ge(S["g5"], b + 1)
                    nc.gpsimd.tensor_tensor(orstd[:], ovare[:], mhalf[:], ALU.pow).then_inc(S["g6"], 1)

            def step(a, bb, m, half):
                if a:
                    rstd_A(*a)
                rstd_M(*m)

            rstd_A(0, 0)
            rstd_A(0, 1)
            walk(pool, step)

        @block.vector
        def _(dve):
            v = nc.vector

            def ln1(l, b):
                if l == 0:
                    if isinstance(b, int) and b < 2:
                        dve.wait_ge(S[f"x_in{b}"], 16)
                    else:
                        dve.wait_ge(S["x_in2"], 16)
                else:
                    dve.wait_ge(S["x_done"], item(l - 1, b))
                v.tensor_reduce(mean[:], x[:, b], AX_X, ALU.add).then_inc(S["ln_sum"], 1)
                dve.wait_ge(S["ln_sum"], item(l, b))
                v.tensor_scalar(mean[:], mean[:], 1.0 / D, None, ALU.mult).then_inc(S["ln_mean"], 1)
                dve.wait_ge(S["ln_mean"], item(l, b))
                v.tensor_tensor(cent[:], x[:, b], spread(mean[:], D), ALU.subtract).then_inc(S["ln_cent"], 1)

            def ln2(l, b):
                dve.wait_ge(S["ln_sq"], item(l, b))
                v.tensor_reduce(var[:], sq[:], AX_X, ALU.add).then_inc(S["ln_ss"], 1)
                dve.wait_ge(S["ln_ss"], item(l, b))
                v.tensor_scalar(vare[:], var[:], 1.0 / D, EPS, ALU.mult, ALU.add).then_inc(S["ln_var"], 1)

            def ln3(l, b, par):
                dve.wait_ge(S["ln_rstd"], item(l, b))
                v.scalar_tensor_tensor(out=h[:, par], in0=cent[:], scalar=0.0, in1=spread(rstd[:], D),
                                       op0=ALU.max, op1=ALU.mult).then_inc(S["h_done"], 1)

            def self_B(l, b, par):
                if l == MEAN:
                    dve.wait_ge(S["hc_done"], b + 1)
                    v.tensor_tensor(selfp[:, par], hc[:, par, :, 0:D], base[:], ALU.add).then_inc(S["self_done"], 1)

            def small1(l, b, par):
                if l in (ATT0, ATT3):
                    s2 = hp[:, par, :, 1]
                    dve.wait_ge(S["hp_done"], att_item(l, b))
                    v.tensor_scalar(s2big[:, par], s2, BIG, None, ALU.mult).then_inc(S["s2big_done"], 1)
                    v.tensor_reduce(smx[:, 0:1], s2, AX_X, ALU.max).then_inc(S["smx_done"], 1)

            def small2(l, b):
                if l == MEAN:
                    return
                r = D if l == CHAN else 1
                n = avg_item(l, b)
                dve.wait_ge(S["mxt_done"], n)
                v.tensor_reduce(mcol[0:r], pj[0:r, 1, 0:P], AX_X, ALU.max).then_inc(S["mcol_done"], 1)
                dve.wait_ge(S["mcol_done"], n)
                v.tensor_scalar(mdiag[0:r, 0:r], ident[0:r, 0:r], mcol[0:r], None, ALU.mult).then_inc(S["mdiag_done"], 1)

            def small3(l, b, par):
                if l not in (ATT0, ATT3):
                    return
                s1, s2 = hp[:, par, :, 0], hp[:, par, :, 1]
                top_s = pj[:, 1, P:P + 1]
                n = att_item(l, b)
                dve.wait_ge(S["mbc_done"], avg_item(l, b))
                v.tensor_scalar(z08[:], s1, top_s, 1.0 - SLOPE, ALU.add, ALU.mult).then_inc(S["z08_done"], 1)
                v.tensor_scalar(pre[:, 0], s2, top_s, 0.5, ALU.subtract, ALU.mult)
                v.tensor_scalar(pre[:, 1], s2, top_s, SLOPE, ALU.subtract, ALU.mult)
                dve.wait_ge(S["z08_done"], n)
                v.tensor_scalar(pre[:, 2], z08[:], 0.0, None, ALU.min)
                v.tensor_scalar(pre[:, 3], z08[:], -1.0, 0.0, ALU.mult, ALU.min).then_inc(S["pre_done"], 1)

            def cmp_B(l, b, par, j0, j1):
                if l not in (ATT0, ATT3):
                    return
                for j in range(j0, j1):
                    dve.wait_ge(S["reach_done"], T * (att_item(l, b) - 1) + j + 1)
                    v.tensor_tensor(C[:, par, j], reach[:, j], maskT[:, j], ALU.min).then_inc(S["c_done"], 1)

            def parts(l, b, par):
                w = width[l]
                dve.wait_ge(S["top_done"], item(l, b))
                v.tensor_tensor(rest[:, par, :, 0:w], top[:, par, :, 0:w], upper(top[:, par])[:, :, 0:w],
                                ALU.subtract).then_inc(S["rest_done"], 1)
                dve.wait_ge(S["rest_done"], item(l, b))
                v.tensor_tensor(low[:, par, :, 0:w], rest[:, par, :, 0:w], upper(rest[:, par])[:, :, 0:w],
                                ALU.subtract).then_inc(S["low_done"], 1)

            def ops_B(l, b, par):
                if l in (ATT0, ATT3):
                    dve.wait_ge(S["ex_done"], att_item(l, b))
                    v.scalar_tensor_tensor(out=vq[:, par, 0], in0=ex[:, par, 0], scalar=BIG, in1=ex[:, par, 0],
                                           op0=ALU.mult, op1=ALU.mult)
                    v.tensor_scalar(vq[:, par, 1], ex[:, par, 1], BIG, None, ALU.mult).then_inc(S["vq_done"], 1)
                    dve.wait_ge(S["vq_done"], att_item(l, b))
                    h1 = hp[:, par, :, 2:2 + V]
                    v.tensor_tensor(top[:, par, :, 0:V], h1, spread(vq[:, par, 0], V), ALU.mult)
                    v.tensor_tensor(top[:, par, :, V:VQ], h1, spread(vq[:, par, 1], V), ALU.mult).then_inc(S["top_done"], 1)
                parts(l, b, par)

            def chan1(l, b, par):
                if l != CHAN:
                    return
                n = b + 1
                dve.wait_ge(S["ln1_done"], n)
                dve.wait_ge(S["rl_done"], n)
                v.tensor_tensor(feat[:, par], rl[:], sp[:], ALU.add).then_inc(S["feat_done"], 1)
                dve.wait_ge(S["feat_done"], n)
                v.tensor_tensor(sc[:], feat[:, par], along(par_row(WA)), ALU.mult).then_inc(S["sc1_done"], 1)
                dve.wait_ge(S["sc1_done"], n)
                v.tensor_tensor(sc[:], sc[:], along(par_row(BA)), ALU.add).then_inc(S["sc_done"], 1)
                dve.wait_ge(S["sc_done"], n)
                v.tensor_reduce(smx[:, 0:D], sc[:].rearrange("p t d -> p d t"), AX_X, ALU.max).then_inc(S["smx_done"], 1)

            def chan2(l, b, par):
                if l != CHAN:
                    return
                n = b + 1
                dve.wait_ge(S["mbc_done"], avg_item(l, b))
                v.tensor_tensor(sc[:], sc[:], along(pj[:, 1, P:P + D]), ALU.subtract).then_inc(S["scm_done"], 1)

            def chan3(l, b, par):
                if l != CHAN:
                    return
                n = b + 1
                dve.wait_ge(S["ee_done"], n)
                v.scalar_tensor_tensor(out=top[:, par, :, D:2 * D], in0=ee[:], scalar=BIG_E, in1=ee[:],
                                       op0=ALU.mult, op1=ALU.mult).then_inc(S["chE_done"], 1)
                dve.wait_ge(S["chE_done"], n)
                v.tensor_tensor(top[:, par, :, 0:D], top[:, par, :, D:2 * D], feat[:, par], ALU.mult).then_inc(S["top_done"], 1)

            def mean_M(l, b):
                if l == MEAN:
                    return
                dve.wait_ge(S["avg_done"], avg_item(l, b))
                v.tensor_copy(hm[:], pj[:, 0, 0:D]).then_inc(S["hm_done"], 1)

            def evac(l, b, par, c):
                t = slice(2 * c, 2 * c + 2)
                bank = acc[:, c, 0:2 * VQ].rearrange("p (t v) -> p t v", v=VQ)
                dve.wait_ge(S["main_done"], CH * (item(l, b) - 1) + c + 1)
                if l in (ATT0, ATT3):
                    v.tensor_tensor(num[:, t, 0:V], bank[:, :, 0:V], spread(ex[:, par, 2, t], V), ALU.mult)
                    v.tensor_tensor(tq[:, t], bank[:, :, V:VQ], spread(ex[:, par, 3, t], V), ALU.mult).then_inc(S["acc_free"], 1)
                if l == MEAN:
                    v.tensor_tensor(num[:, t, 0:D], bank[:, :, 0:D], spread(rdeg[:, t], D), ALU.mult).then_inc(S["acc_free"], 1)
                if l == CHAN:
                    v.tensor_copy(num[:, t, 0:D], bank[:, :, 0:D])
                    v.tensor_tensor(num[:, t, D:2 * D], bank[:, :, D:2 * D], spread(lone[:, t], D), ALU.add).then_inc(S["acc_free"], 1)

            def add_lonely(l, b):
                n = avg_item(l, b)
                dve.wait_ge(S["hm_done"], n)
                v.tensor_tensor(lz[:], along(hm[:]), spread(lone[:], D), ALU.mult).then_inc(S["lz_done"], 1)
                dve.wait_ge(S["att1"], n)
                dve.wait_ge(S["lz_done"], n)
                v.tensor_tensor(att[:], att[:], lz[:], ALU.add).then_inc(S["att_done"], 1)
                dve.wait_ge(S["att_done"], n)

            def final(l, b, par):
                n = att_item(l, b)
                xb = x[:, b]
                dve.wait_ge(S["acc_free"], freed(l, b, CH))
                if l in (ATT0, ATT3):
                    v.tensor_tensor(num[:, :, 0:V], num[:, :, 0:V], tq[:], ALU.subtract).then_inc(S["num_done"], 1)
                    dve.wait_ge(S["num_done"], n)
                    v.tensor_tensor(rden[:, :, 0], num[:, :, D], lone[:], ALU.add).then_inc(S["den_done"], 1)
                    dve.wait_ge(S["den_done"], n)
                    v.reciprocal(rden[:, :, 1], rden[:, :, 0]).then_inc(S["rden_done"], 1)
                    dve.wait_ge(S["rden_done"], avg_item(l, b))
                    v.tensor_tensor(att[:], num[:, :, 0:D], spread(rden[:, :, 1], D), ALU.mult).then_inc(S["att1"], 1)
                    add_lonely(l, b)
                if l == ATT0:
                    v.tensor_scalar(neg[:], att[:], 0.0, None, ALU.min).then_inc(S["neg_done"], 1)
                    dve.wait_ge(S["en_done"], b + 1)
                    v.scalar_tensor_tensor(out=so[:], in0=att[:], scalar=0.0, in1=en[:], op0=ALU.max, op1=ALU.add)\
                        .then_inc(S["so_done"], 1)
                    dve.wait_ge(S["so_done"], b + 1)
                    v.scalar_tensor_tensor(out=xb, in0=so[:], scalar=-1.0, in1=xb, op0=ALU.add, op1=ALU.add)\
                        .then_inc(S["x_done"], 1)
                if l == ATT3:
                    v.scalar_tensor_tensor(out=xb, in0=att[:], scalar=0.0, in1=xb, op0=ALU.max, op1=ALU.add)\
                        .then_inc(S["x_done"], 1)
                if l == CHAN:
                    v.reciprocal(rden[:], num[:, :, D:2 * D]).then_inc(S["rden_done"], 1)
                    dve.wait_ge(S["rden_done"], avg_item(l, b))
                    v.tensor_tensor(att[:], num[:, :, 0:D], rden[:], ALU.mult).then_inc(S["att1"], 1)
                    add_lonely(l, b)
                    v.tensor_tensor(xb, att[:], xb, ALU.add).then_inc(S["x_done"], 1)
                if l == MEAN:
                    n = b + 1
                    v.tensor_tensor(so[:], num[:, :, 0:D], selfp[:, par], ALU.add).then_inc(S["g1"], 1)
                    dve.wait_ge(S["g1"], n)
                    v.tensor_scalar(so[:], so[:], 0.0, None, ALU.max).then_inc(S["g2"], 1)
                    dve.wait_ge(S["g2"], n)
                    v.tensor_reduce(osum[:], so[:], AX_X, ALU.add).then_inc(S["g3"], 1)
                    dve.wait_ge(S["g3"], n)
                    v.tensor_scalar(osum[:], osum[:], 1.0 / D, None, ALU.mult).then_inc(S["g11"], 1)
                    dve.wait_ge(S["g11"], n)
                    v.tensor_tensor(oc[:], so[:], spread(osum[:], D), ALU.subtract).then_inc(S["g4"], 1)
                    dve.wait_ge(S["g4"], n)
                    v.tensor_tensor(osq[:], oc[:], oc[:], ALU.mult).then_inc(S["g7"], 1)
                    dve.wait_ge(S["g7"], n)
                    v.tensor_reduce(ovar[:], osq[:], AX_X, ALU.add).then_inc(S["g8"], 1)
                    dve.wait_ge(S["g8"], n)
                    v.tensor_scalar(ovare[:], ovar[:], 1.0 / D, EPS, ALU.mult, ALU.add).then_inc(S["g5"], 1)
                    dve.wait_ge(S["g6"], n)
                    v.tensor_tensor(oc[:], oc[:], spread(orstd[:], D), ALU.mult).then_inc(S["g9"], 1)
                    dve.wait_ge(S["g9"], n)
                    v.tensor_tensor(oc[:], oc[:], along(par_row(GAMMA)), ALU.mult).then_inc(S["g10"], 1)
                    dve.wait_ge(S["g10"], n)
                    v.tensor_tensor(oc[:], oc[:], along(par_row(BETA)), ALU.add).then_inc(S["so_done"], 1)
                    dve.wait_ge(S["so_done"], B + n)
                    v.tensor_tensor(xb, oc[:], xb, ALU.add).then_inc(S["x_done"], 1)

            def step(a, bb, m, half):
                if a:
                    ln1(*a)
                if bb:
                    small1(*bb, 1 - half)
                    chan1(*bb, 1 - half)
                mean_M(*m)
                if a:
                    ln2(*a)
                if bb:
                    cmp_B(*bb, 1 - half, 0, T // 4)
                evac(*m, half, 0)
                if bb:
                    small2(*bb)
                if a:
                    ln3(*a, half)
                if bb:
                    cmp_B(*bb, 1 - half, T // 4, T // 2)
                evac(*m, half, 1)
                if bb:
                    small3(*bb, 1 - half)
                    chan2(*bb, 1 - half)
                    cmp_B(*bb, 1 - half, T // 2, T)
                evac(*m, half, 2)
                if bb:
                    chan3(*bb, 1 - half)
                    self_B(*bb, 1 - half)
                    ops_B(*bb, 1 - half)
                evac(*m, half, 3)
                final(*m, half)

            for g in range(2):
                dve.wait_ge(S["w_in"], W_IN)
                v.tensor_copy(arep[g][:], acol[g][:, 0:1].to_broadcast([D, P])).then_inc(S["arep_sb"], 1)
            for g in range(2):
                dve.wait_ge(S["wt_ps"], g + 1)
                v.tensor_copy(wtr[g][:], acc[0:D, g, 0:D]).then_inc(S["wt_sb"], 1)
            dve.wait_ge(S["rows_ps"], 1)
            v.tensor_copy(par_rows[:], acc[:, 2, 0:NR * D + 2]).then_inc(S["rows_sb"], 1)
            dve.wait_ge(S["rows_sb"], 1)
            v.tensor_scalar(k0[:], par_rows[:, NR * D:NR * D + 1], 0.7071067811865476, None, ALU.mult)
            v.tensor_copy(b0[:], par_rows[:, NR * D + 1:NR * D + 2]).then_inc(S["scal_sb"], 1)
            for g in range(2):
                dve.wait_ge(S["wa_ps"], g + 1)
                for half in range(2):
                    q = slice(half * D, half * D + D)
                    v.tensor_copy(wext[g][q, 0:2], acc[0:D, g, 128:130])
                    v.tensor_copy(w1rep[g][q], acc[0:D, g, 256:256 + P])
                    last = v.tensor_copy(wext[g][q, 2:G], wnat[g][:] if g == 0 else wtr[g][:])
                last.then_inc(S["wa_sb"], 1)
            dve.wait_ge(S["const_g"], 1)
            ln1(0, 0)
            ln2(0, 0)
            ln3(0, 0, 0)
            ln1(0, 1)
            ln2(0, 1)
            small1(0, 0, 0)
            small2(0, 0)
            small3(0, 0, 0)
            ln3(0, 1, 1)
            dve.wait_ge(S["adj_in"], 16)
            for t in range(T):
                v.tensor_scalar(mask[:, t], adj[:, t], 0.0, None, ALU.is_gt).then_inc(S["mask_nat"], 1)
            for t in range(T):
                dve.wait_ge(S["mask_tr"], t + 1)
                v.tensor_copy(maskT[:, :, t * P:(t + 1) * P],
                              acc[:, t % CH].bitcast(BF16).rearrange("p (j i) -> p j i", i=P)).then_inc(S["acc_free"], 1)
            dve.wait_ge(S["acc_free"], T)
            dve.wait_ge(S["deg_sb"], T)
            for t in range(T):
                v.tensor_scalar(nmaskT[:, t], maskT[:, t], -1.0, None, ALU.mult).then_inc(S["nmask_sb"], 1)
            v.tensor_scalar(lone[:], deg[:], 0.0, None, ALU.is_equal)
            v.tensor_scalar(some[:], deg[:], 0.0, None, ALU.is_gt)
            v.tensor_scalar(deg1[:], deg[:], 1.0, None, ALU.max).then_inc(S["deg1_sb"], 1)
            dve.wait_ge(S["deg1_sb"], 1)
            v.reciprocal(rdeg[:], deg1[:])
            v.tensor_tensor(base[:], along(par_row(B_NEIGH)), spread(some[:], D), ALU.mult).then_inc(S["base_sb"], 1)
            dve.wait_ge(S["base_sb"], 1)
            v.tensor_tensor(base[:], base[:], along(par_row(B_SELF)), ALU.add).then_inc(S["base2_sb"], 1)
            dve.wait_ge(S["base2_sb"], 1)
            cmp_B(0, 0, 0, 0, T)
            ops_B(0, 0, 0)
            walk(dve, step)

        @block.scalar
        def _(act):
            s = nc.scalar

            def sq_A(l, b):
                act.wait_ge(S["ln_cent"], item(l, b))
                s.activation(sq[:], cent[:], ACT.Square).then_inc(S["ln_sq"], 1)

            def hT_A(l, b):
                if l == CHAN:
                    return
                act.wait_ge(S["tr_done"], tr_item(l, b))
                s.activation(hT[:].rearrange("p k n -> p (k n)"), tp[:, 0], ACT.Copy).then_inc(S["hT_done"], 1)

            def hp_A(l, b, par):
                if l in (ATT0, ATT3):
                    act.wait_ge(S["pj_done"], tr_item(l, b))
                    s.activation(hp[:, par, :, 0:G].rearrange("p (t k) g -> p k t g", k=2),
                                 pj[:, :, 0:T // 2 * G].rearrange("p k (t g) -> p k t g", g=G), ACT.Copy)\
                        .then_inc(S["hp_done"], 1)
                if l == MEAN:
                    act.wait_ge(S["pj_done"], tr_item(l, b))
                    s.activation(hc[:, par].rearrange("p (t k) g -> p k t g", k=2),
                                 pj[:].rearrange("p k (t g) -> p k t g", g=2 * D), ACT.Copy).then_inc(S["hc_done"], 1)

            def top_B(l, b, par):
                if l == MEAN:
                    act.wait_ge(S["hc_done"], b + 1)
                    s.activation(top[:, par, :, 0:D], hc[:, par, :, D:2 * D], ACT.Copy).then_inc(S["top_done"], 1)

            def s1_A(l, b):
                if l in (ATT0, ATT3):
                    if not (l == 0 and isinstance(b, int) and b == 0):
                        act.wait_ge(S["reach_done"], T * (att_item(l, b) - 1))
                    act.wait_ge(S["s1_done"], att_item(l, b))
                    s.activation(s1bc[:].rearrange("p (t k n) -> p k t n", k=2, n=P),
                                 tp[:].rearrange("p k (t n) -> p k t n", n=P), ACT.Copy).then_inc(S["s1bc_done"], 1)

            def ex_B(l, b, par):
                if l in (ATT0, ATT3):
                    act.wait_ge(S["pre_done"], att_item(l, b))
                    s.activation(ex[:, par], pre[:], ACT.Exp).then_inc(S["ex_done"], 1)

            def reach_B(l, b, par, j0, j1):
                if l not in (ATT0, ATT3):
                    return
                n = att_item(l, b)
                if j0 == 0:
                    act.wait_ge(S["s2big_done"], n)
                    act.wait_ge(S["s1bc_done"], n)
                    act.wait_ge(S["mask_tr"], T)
                    act.wait_ge(S["deg_sb"], T)
                for j in range(j0, j1):
                    s.activation(reach[:, j], s1bc[:], ACT.Relu, scale=BIG, bias=s2big[:, par, j:j + 1])\
                        .then_inc(S["reach_done"], 1)

            def soft_B(l, b, par):
                if l != CHAN:
                    return
                n = b + 1
                act.wait_ge(S["h_done"], item(l, b))
                s.activation(ab[:], h[:, par], ACT.Abs, scale=k0[:], bias=b0[:]).then_inc(S["ab_done"], 1)
                s.activation(rl[:], h[:, par], ACT.Relu, scale=k0[:], bias=b0[:]).then_inc(S["rl_done"], 1)
                act.wait_ge(S["ab_done"], n)
                s.activation(sp[:], ab[:], ACT.Exp, scale=-1.0).then_inc(S["e1_done"], 1)
                act.wait_ge(S["e1_done"], n)
                s.activation(sp[:], sp[:], ACT.Ln, bias=1.0).then_inc(S["ln1_done"], 1)

            def ee_B(l, b):
                if l == CHAN:
                    act.wait_ge(S["scm_done"], b + 1)
                    s.activation(ee[:], sc[:], ACT.Exp, scale=0.5).then_inc(S["ee_done"], 1)

            def elu_M(l, b):
                if l == ATT0:
                    act.wait_ge(S["neg_done"], b + 1)
                    s.activation(en[:], neg[:], ACT.Exp).then_inc(S["en_done"], 1)

            def step(a, bb, m, half):
                if a:
                    sq_A(*a)
                if bb:
                    soft_B(*bb, 1 - half)
                    top_B(*bb, 1 - half)
                    reach_B(*bb, 1 - half, 0, 5)
                if a:
                    hT_A(*a)
                if bb:
                    reach_B(*bb, 1 - half, 5, T)
                    ex_B(*bb, 1 - half)
                    ee_B(*bb)
                if a:
                    hp_A(*a, half)
                    s1_A(*a)
                elu_M(*m)

            sq_A(0, 0)
            hT_A(0, 0)
            hp_A(0, 0, 0)
            s1_A(0, 0)
            sq_A(0, 1)
            ex_B(0, 0, 0)
            hT_A(0, 1)
            hp_A(0, 1, 1)
            for t in range(T):
                act.wait_ge(S["mask_nat"], t + 1)
                s.activation(nmaskT[:, t], mask[:, t], ACT.Copy, accum_out=deg[:, t:t + 1]).then_inc(S["deg_sb"], 1)
            reach_B(0, 0, 0, 0, T)
            s1_A(0, 1)
            walk(act, step)

        @block.tensor
        def _(pe):
            mm = nc.tensor.matmul

            def tr_A(l, b, par):
                if l == CHAN:
                    return
                if not (l == 0 and isinstance(b, int) and b == 0):
                    pe.wait_ge(S["s1bc_done"], B if l == MEAN else att_item(l, b) - 1)
                pe.wait_ge(S["h_done"], item(l, b))
                for t in range(T // 2):
                    last = nc.tensor.transpose(tp[:, 0, t * P:(t + 1) * P],
                                               h[:, par, 2 * t:2 * t + 2].rearrange("p t d -> p (t d)"), ident[:])
                last.then_inc(S["tr_done"], 1)

            def proj_A(l, b):
                if l == CHAN:
                    return
                w = wconv if l == MEAN else wext[l // 3]
                g = 2 * D if l == MEAN else G
                if l == MEAN and not (isinstance(b, int) and b == 0):
                    pe.wait_ge(S["hc_done"], b)
                pe.wait_ge(S["hT_done"], tr_item(l, b))
                for t in range(T):
                    q = slice(t % 2 * D, t % 2 * D + D)
                    last = mm(pj[:, t % 2, (t // 2) * g:(t // 2 + 1) * g], hT[q, t // 2], w[q, 0:g], start=True, stop=True)
                last.then_inc(S["pj_done"], 1)

            def s1_A(l, b):
                if l in (ATT0, ATT3):
                    for k in range(2):
                        q = slice(k * D, k * D + D)
                        last = mm(tp[:, k], w1rep[l // 3][q], hT[q].rearrange("p t n -> p (t n)"), start=True, stop=True)
                    last.then_inc(S["s1_done"], 1)

            def mean_M(l, b, par):
                if l == MEAN:
                    return
                if l == ATT0 and isinstance(b, int) and b == B - 1:
                    pe.wait_ge(S["hc_done"], 1)
                elif l == ATT0 or (l == ATT3 and not (isinstance(b, int) and b == B - 1)):
                    pe.wait_ge(S["hp_done"], att_item(l, b) + 1)
                elif l == CHAN and isinstance(b, int) and b == B - 1:
                    pe.wait_ge(S["hp_done"], B + 1)
                for t in range(T):
                    r = feat[:, par, t] if l == CHAN else hp[:, par, t, 2:2 + D]
                    last = mm(pj[:, 0, 0:D], avg[:], r, start=(t == 0), stop=(t == T - 1))
                last.then_inc(S["avg_done"], 1)

            def mxt_B(l, b):
                if l != MEAN:
                    pe.wait_ge(S["smx_done"], avg_item(l, b))
                    nc.tensor.transpose(pj[:, 1, 0:P], smx[:], ident[:]).then_inc(S["mxt_done"], 1)

            def mbc_B(l, b):
                if l != MEAN:
                    r = D if l == CHAN else 1
                    pe.wait_ge(S["mdiag_done"], avg_item(l, b))
                    mm(pj[:, 1, P:P + r], ones[0:r], mdiag[0:r, 0:r], start=True, stop=True).then_inc(S["mbc_done"], 1)

            def main(l, b, par, c):
                w = width[l]
                if c == 0:
                    pe.wait_ge(S["low_done"], item(l, b))
                    if l in (ATT0, ATT3):
                        pe.wait_ge(S["c_done"], T * att_item(l, b))
                pe.wait_ge(S["acc_free"], freed(l, b, c + 1 - CH))
                cuts = (upper(top[:, par]), upper(rest[:, par]), low[:, par])
                for i in range(2 * c, 2 * c + 2):
                    o = (i % 2) * VQ
                    rowt = slice(i * P, (i + 1) * P)
                    if l in (ATT0, ATT3):
                        for j in range(T):
                            for s_ in range(3):
                                mm(acc[:, c, o:o + VQ], C[:, par, j, rowt], cuts[s_][:, j], start=(j == 0 and s_ == 0), stop=False)
                        for j in range(T):
                            for s_ in range(3):
                                last = mm(acc[:, c, o + V:o + VQ], nmaskT[:, j, rowt], cuts[s_][:, j, V:VQ],
                                          start=False, stop=(j == T - 1 and s_ == 2))
                    else:
                        for j in range(T):
                            for s_ in range(3):
                                last = mm(acc[:, c, o:o + w], maskT[:, j, rowt], cuts[s_][:, j, 0:w],
                                          start=(j == 0 and s_ == 0), stop=(j == T - 1 and s_ == 2))
                last.then_inc(S["main_done"], 1)

            def step(a, bb, m, half):
                mean_M(*m, half)
                main(*m, half, 0)
                if bb:
                    mxt_B(*bb)
                main(*m, half, 1)
                if bb:
                    mbc_B(*bb)
                if a:
                    tr_A(*a, half)
                main(*m, half, 2)
                if a:
                    if m[0] != MEAN:
                        pe.wait_ge(S["hm_done"], avg_item(*m))
                    if bb[0] == CHAN:
                        pe.wait_ge(S["scm_done"], bb[1] + 1)
                    if bb[0] in (ATT0, ATT3):
                        pe.wait_ge(S["pre_done"], att_item(*bb))
                    proj_A(*a)
                main(*m, half, 3)
                if a:
                    s1_A(*a)

            pe.wait_ge(S["identb_g"], 1)
            pe.wait_ge(S["w_in"], W_IN)
            for g in range(2):
                nc.tensor.transpose(acc[0:D, g, 0:D], wnat[g][:], ident[0:D, 0:D]).then_inc(S["wt_ps"], 1)
            mm(acc[:, 2, 0:NR * D + 2], ones[0:1, :], rows[:], start=True, stop=True).then_inc(S["rows_ps"], 1)
            pe.wait_ge(S["arep_sb"], 2)
            for g in range(2):
                pe.wait_ge(S["wt_sb"], g + 1)
                w = wtr[g] if g == 0 else wnat[g]
                mm(acc[0:D, g, 128:130], w[:], acol[g][:], start=True, stop=True)
                mm(acc[0:D, g, 256:256 + P], w[:], arep[g][:], start=True, stop=True).then_inc(S["wa_ps"], 1)
            pe.wait_ge(S["wa_sb"], 2)
            tr_A(0, 0, 0)
            proj_A(0, 0)
            s1_A(0, 0)
            mxt_B(0, 0)
            mbc_B(0, 0)
            tr_A(0, 1, 1)
            pe.wait_ge(S["pre_done"], 1)
            proj_A(0, 1)
            for t in range(T):
                pe.wait_ge(S["mask_nat"], t + 1)
                if t >= CH:
                    pe.wait_ge(S["acc_free"], t - CH + 1)
                for j in range(T):
                    last = nc.tensor.transpose(acc[:, t % CH].bitcast(BF16)[:, j * P:(j + 1) * P],
                                               mask[:, t].rearrange("p (q j) -> p j q", j=T)[:, j], identb[:])
                last.then_inc(S["mask_tr"], 1)
            s1_A(0, 1)
            pe.wait_ge(S["nmask_sb"], T)
            walk(pe, step)


_WEIGHTS = ['L0_gnn_W', 'L0_gnn_a', 'L1_gnn_W_self', 'L1_gnn_b_self', 'L1_gnn_W_neigh', 'L1_gnn_b_neigh',
            'L1_gnn_ln_gamma', 'L1_gnn_ln_beta', 'L2_gnn_w0', 'L2_gnn_b0', 'L2_gnn_wa', 'L2_gnn_ba',
            'L3_gnn_W', 'L3_gnn_a']


def kernel(**inputs):
    import numpy as _np
    import concourse.bacc as _bacc
    from concourse import mybir as _mybir
    from concourse.bass_utils import run_bass_kernel_spmd as _run

    nc = _bacc.Bacc("TRN2", target_bir_lowering=False, num_devices=1)
    arrays, aps = {}, {}
    for name in ['x', 'adj'] + _WEIGHTS:
        a = _np.ascontiguousarray(inputs[name])
        arrays[f"in_{name}"] = a
        aps[name] = nc.dram_tensor(f"in_{name}", a.shape, _mybir.dt.from_np(a.dtype), kind="ExternalInput").ap()
    o = nc.dram_tensor("out_x", inputs['x'].shape, _mybir.dt.float32, kind="ExternalOutput").ap()
    build(nc, aps['x'], aps['adj'], {n: aps[n] for n in _WEIGHTS}, o)
    r = _run(nc, [arrays], core_ids=[0])
    return r.results[0]["out_x"]
```

```python
from contextlib import ExitStack

import concourse.bass as bass
from concourse import mybir

ALU = mybir.AluOpType
ACT = mybir.ActivationFunctionType
F32 = mybir.dt.float32
BF16 = mybir.dt.bfloat16
I32 = mybir.dt.int32
AX_X = mybir.AxisListType.X


P = 128
ATT0, MEAN, CHAN, ATT3 = range(4)
LAYERS = 4
EPS = 1e-5
SLOPE = 0.2
BIG = float(2.0 ** 100)
BIG_E = float(2.0 ** 80)


def build(nc, x_in, adj_in, w_in, out):
    B, N, D = x_in.shape
    T = N // P
    G = D + 2
    V = D + 1
    VQ = 2 * V
    CH = T // 2
    NR = 6

    with ExitStack() as ctx:
        def sb(name, shape, dt=F32):
            return ctx.enter_context(nc.sbuf_tensor(name, shape, dt))

        def ps(name, shape):
            return ctx.enter_context(nc.psum_tensor(name, shape, F32))

        def sem(name):
            return ctx.enter_context(nc.semaphore(name))

        x = sb("x", [P, B, T, D])
        maskT = sb("maskT", [P, T, N], BF16)
        nmaskT = sb("nmaskT", [P, T, N], BF16)
        deg = sb("deg", [P, T])
        deg1 = sb("deg1", [P, T])
        rdeg = sb("rdeg", [P, T])
        lone = sb("lone", [P, T])
        some = sb("some", [P, T])
        base = sb("base", [P, T, D])
        ones = sb("ones", [P, P])
        ident = sb("ident", [P, P])
        identb = sb("identb", [P, P], BF16)
        avg = sb("avg", [P, 1])
        mhalf = sb("mhalf", [P, T])
        rows = sb("rows", [1, NR * D + 2])
        par_rows = sb("par_rows", [P, NR * D + 2])
        k0 = sb("k0", [P, 1])
        b0 = sb("b0", [P, 1])
        wnat = [sb(f"wnat{g}", [D, D]) for g in range(2)]
        wtr = [sb(f"wtr{g}", [D, D]) for g in range(2)]
        acol = [sb(f"acol{g}", [D, 2]) for g in range(2)]
        arep = [sb(f"arep{g}", [D, P]) for g in range(2)]
        wext = [sb(f"wext{g}", [P, 2 * G]) for g in range(2)]
        wconv = sb("wconv", [P, 4 * D])
        w1rep = [sb(f"w1rep{g}", [P, P]) for g in range(2)]
        lnsum = sb("lnsum", [P, T])
        cent = sb("cent", [P, T, D])
        sq = sb("sq", [P, T, D])
        var = sb("var", [P, T])
        vare = sb("vare", [P, T])
        rstd = sb("rstd", [P, T])
        h = sb("h", [P, 2, T, D])
        hT = sb("hT", [P, T // 2, P])
        hp = sb("hp", [P, 2, T, G + 2])
        s1bc = sb("s1bc", [P, N])
        hc = sb("hc", [P, 2, T, 2 * D])
        ab = sb("ab", [P, T, D])
        rl = sb("rl", [P, T, D])
        sp = sb("sp", [P, T, D])
        feat = sb("feat", [P, 2, T, D])
        sc = sb("sc", [P, 2, T, D])
        selfp = sb("selfp", [P, 2, T, D])
        smx = sb("smx", [P, P])
        mcol = sb("mcol", [D, 1])
        diag = sb("diag", [D, 2 * D])
        hm = sb("hm", [P, 2, D])
        s2big = sb("s2big", [P, 2, T])
        z08 = sb("z08", [P, T])
        pre = sb("pre", [P, 4, T])
        ex = sb("ex", [P, 2, 4, T])
        vq = sb("vq", [P, 2, T])
        ee = sb("ee", [P, T, D])
        reach = sb("reach", [P, T, N], BF16)
        C = sb("C", [P, 2, T, N], BF16)
        adj = C[:].rearrange("p a t n -> p (a t n)").bitcast(I32).rearrange("p (t n) -> p t n", t=T)
        mask = nmaskT
        top = sb("top", [P, 2, T, VQ])
        rest = sb("rest", [P, 2, T, VQ])
        low = sb("low", [P, 2, T, VQ], BF16)
        count_bin = rest[:, 1].rearrange("p t v -> p (t v)").bitcast(BF16)[:, 0:N]
        num = sb("num", [P, 2, T, VQ])
        den = sb("den", [P, T])
        rden = sb("rden", [P, T, D])
        att = sb("att", [P, T, D])
        neg = sb("neg", [P, T, D])
        en = sb("en", [P, T, D])
        so = sb("so", [P, T, D])
        conv = sb("conv", [P, T, D])
        sr = sb("sr", [P, T, D])
        osum = sb("osum", [P, T])
        ovar = sb("ovar", [P, T])
        ovare = sb("ovare", [P, T])
        orstd = sb("orstd", [P, T])
        oc = sb("oc", [P, T, D])
        osq = sb("osq", [P, T, D])

        acc = ps("acc", [P, CH, 512])
        tp = ps("tp", [P, 2, 512])
        pj = ps("pj", [P, 2, 512])
        MEANS = P
        MAXIMA = P + D

        names = """x_in0 x_in1 x_in2 w_in const_g ident_g identb_g rows_ps rows_sb wt_ps wt_sb arep_sb wa_ps wa_sb
            mask_nat mask_tr acc_free nmask_sb deg_sb deg1_sb base_sb base2_sb scal_sb
            ln_sum ln_cent ln_sq ln_ss ln_var ln_rstd h_done tr_done hT_done pj_done s1_done hp_done s1bc_done hc_done
            ab_done e1_done ln1_done rl_done feat_done sc1_done sc_done
            self_done smx_done mxt_done mcol_done diag_done mbc_done hm_done s2big_done z08_done pre_done ex_done
            vq_done reach_done c_done scm_done ee_done chE_done topcopy_done top_done rest_done low_done main_done
            diff_done den_done rden_done att_done filled_done neg_done en_done elu_done
            conv_done conv_relu_done osum_done ocent_done osq_done oss_done ovar_done orstd_done
            onorm_done ogamma_done obeta_done x_done out_done""".split() + [f"adj_in{t}" for t in range(T)]
        S = {n: sem(n) for n in names}

        def item(l, b):
            return B * l + b + 1

        def att_item(l, b):
            return B * (l // 3) + b + 1

        def avg_item(l, b):
            return B * (0, 0, 1, 2)[l] + b + 1

        def tr_item(l, b):
            return B * (0, 1, 1, 2)[l] + b + 1

        def freed(l, b, c):
            return T + CH * (item(l, b) - 1) + c

        def upper(t):
            return t.bitcast(BF16).rearrange("p t (v two) -> p t v two", two=2)[:, :, :, 1]

        def spread(t, d):
            return t.unsqueeze(2).to_broadcast([P, t.shape[1], d])

        def along(r):
            return r.unsqueeze(1).to_broadcast([P, T, r.shape[1]])

        width = (VQ, D, 2 * D, VQ)
        ATT = (ATT0, ATT3)

        def very_first(it):
            return isinstance(it[1], int) and it == (0, 0)

        def par_row(n):
            return par_rows[:, n * D:(n + 1) * D]

        B_SELF, B_NEIGH, GAMMA, BETA, WA, BA = range(NR)

        def walk(step):
            def walk_layer(l, fori):
                nxt = (lambda b: (l + 1, b)) if l + 1 < LAYERS else (lambda b: None)
                step((l, 2), (l, 1), (l, 0), (l - 1, B - 1) if l else None, 0)
                step((l, 3), (l, 2), (l, 1), (l, 0), 1)
                with fori(2, B - 3, 2) as b:
                    step((l, b + 2), (l, b + 1), (l, b), (l, b - 1), 0)
                    step((l, b + 3), (l, b + 2), (l, b + 1), (l, b), 1)
                step(nxt(0), (l, B - 1), (l, B - 2), (l, B - 3), 0)
                step(nxt(1), nxt(0), (l, B - 1), (l, B - 2), 1)
            return walk_layer

        def run(eng, step):
            walk_layer = walk(step)
            for l in range(LAYERS):
                walk_layer(l, eng.Fori)
            step(None, None, None, (LAYERS - 1, B - 1), 0)

        block = ctx.enter_context(nc.Block())

        @block.sync
        def _(sync):
            xv = x_in.rearrange("b (p t) d -> p b (t d)", t=T)
            xs = x[:].rearrange("p b t d -> p b (t d)")
            sync.dma_start(xs[:, 0:1], xv[:, 0:1]).then_inc(S["x_in0"], 16)
            for g, (w, a) in enumerate(((w_in["L0_gnn_W"], w_in["L0_gnn_a"]), (w_in["L3_gnn_W"], w_in["L3_gnn_a"]))):
                sync.dma_start(wnat[g][:], w).then_inc(S["w_in"], 16)
                for c in range(2):
                    sync.dma_start(acol[g][:, c:c + 1], a[c * D:(c + 1) * D, :]).then_inc(S["w_in"], 16)
            for n, name in enumerate(("L1_gnn_b_self", "L1_gnn_b_neigh", "L1_gnn_ln_gamma", "L1_gnn_ln_beta",
                                      "L2_gnn_wa", "L2_gnn_ba")):
                sync.dma_start(rows[0:1, n * D:(n + 1) * D], w_in[name].rearrange("(o d) -> o d", o=1)).then_inc(S["w_in"], 16)
            sync.dma_start(rows[0:1, NR * D:NR * D + 1], w_in["L2_gnn_w0"]).then_inc(S["w_in"], 16)
            sync.dma_start(rows[0:1, NR * D + 1:NR * D + 2],
                           w_in["L2_gnn_b0"].rearrange("(o d) -> o d", o=1)).then_inc(S["w_in"], 16)
            sync.wait_ge(S["const_g"], 1)
            for half in range(2):
                q, o = slice(half * D, half * D + D), half * 2 * D
                sync.dma_start(wconv[q, o:o + D], w_in["L1_gnn_W_self"]).then_inc(S["w_in"], 16)
                sync.dma_start(wconv[q, o + D:o + 2 * D], w_in["L1_gnn_W_neigh"]).then_inc(S["w_in"], 16)
            sync.dma_start(xs[:, 1:2], xv[:, 1:2]).then_inc(S["x_in1"], 16)
            sync.dma_start(xs[:, 2:B], xv[:, 2:B]).then_inc(S["x_in2"], 16)
            ov = out.rearrange("b (p t) d -> p b (t d)", t=T)
            for b in range(B):
                sync.wait_ge(S["x_done"], item(ATT3, b))
                sync.dma_start(ov[:, b:b + 1], xs[:, b:b + 1]).then_inc(S["out_done"], 16)
            sync.wait_ge(S["out_done"], 16 * B)
        W_IN = 16 * 18

        @block.gpsimd
        def _(pool):
            g = nc.gpsimd
            g.memset(ones[:], 1.0)
            g.memset(avg[:], 1.0 / N)
            g.memset(mhalf[:], -0.5)
            g.memset(smx[:], 0.0)
            g.memset(wext[0][:], 0.0)
            g.memset(wext[1][:], 0.0)
            g.memset(wconv[:], 0.0)
            g.memset(hp[:, :, :, G:G + 1], 1.0)
            g.memset(ident[:], 0.0).then_inc(S["const_g"], 1)
            pool.wait_ge(S["const_g"], 1)
            g.affine_select(out=ident[:], in_=ident[:], compare_op=ALU.not_equal, fill=1.0, base=0,
                            pattern=[[-1, P]], channel_multiplier=1).then_inc(S["ident_g"], 1)
            pool.wait_ge(S["ident_g"], 1)
            g.tensor_copy(identb[:], ident[:]).then_inc(S["identb_g"], 1)

            def rstd_A(a):
                if not a:
                    return
                pool.wait_ge(S["ln_var"], item(*a))
                g.tensor_tensor(rstd[:], vare[:], mhalf[:], ALU.pow).then_inc(S["ln_rstd"], 1)

            def rstd_F(f):
                if not f or f[0] != MEAN:
                    return
                pool.wait_ge(S["ovar_done"], f[1] + 1)
                g.tensor_tensor(orstd[:], ovare[:], mhalf[:], ALU.pow).then_inc(S["orstd_done"], 1)

            def step(a, b, m, f, half):
                rstd_A(a)
                rstd_F(f)

            rstd_A((0, 0))
            rstd_A((0, 1))
            run(pool, step)

        @block.vector
        def _(dve):
            v = nc.vector

            def sum_A(a):
                if not a:
                    return
                l, b = a
                if l == 0:
                    dve.wait_ge(S[f"x_in{b}" if isinstance(b, int) and b < 2 else "x_in2"], 16)
                else:
                    dve.wait_ge(S["x_done"], item(l - 1, b))
                v.tensor_reduce(lnsum[:], x[:, b], AX_X, ALU.add).then_inc(S["ln_sum"], 1)

            def cent_A(a):
                if not a:
                    return
                dve.wait_ge(S["ln_sum"], item(*a))
                v.scalar_tensor_tensor(out=cent[:], in0=spread(lnsum[:], D), scalar=-1.0 / D, in1=x[:, a[1]],
                                       op0=ALU.mult, op1=ALU.add).then_inc(S["ln_cent"], 1)

            def var_A(a):
                if not a:
                    return
                dve.wait_ge(S["ln_sq"], item(*a))
                v.tensor_reduce(var[:], sq[:], AX_X, ALU.add).then_inc(S["ln_ss"], 1)
                dve.wait_ge(S["ln_ss"], item(*a))
                v.tensor_scalar(vare[:], var[:], EPS, None, ALU.add).then_inc(S["ln_var"], 1)

            def h_A(a, par):
                if not a:
                    return
                dve.wait_ge(S["ln_rstd"], item(*a))
                v.scalar_tensor_tensor(out=h[:, par], in0=cent[:], scalar=0.0, in1=spread(rstd[:], D),
                                       op0=ALU.max, op1=ALU.mult).then_inc(S["h_done"], 1)

            def feat_A(a, par):
                if not a or a[0] != CHAN:
                    return
                n = a[1] + 1
                dve.wait_ge(S["ln1_done"], n)
                v.tensor_tensor(feat[:, par], rl[:], sp[:], ALU.add).then_inc(S["feat_done"], 1)
                dve.wait_ge(S["feat_done"], n)
                v.tensor_tensor(sc[:, par], feat[:, par], along(par_row(WA)), ALU.mult).then_inc(S["sc1_done"], 1)
                dve.wait_ge(S["sc1_done"], n)
                v.tensor_tensor(sc[:, par], sc[:, par], along(par_row(BA)), ALU.add).then_inc(S["sc_done"], 1)

            def max_B(b, par):
                if not b or b[0] == MEAN:
                    return
                if b[0] in ATT:
                    s2 = hp[:, par, :, 1]
                    dve.wait_ge(S["hp_done"], att_item(*b))
                    v.tensor_scalar(s2big[:, par], s2, BIG, None, ALU.mult).then_inc(S["s2big_done"], 1)
                    v.tensor_reduce(smx[:, 0:1], s2, AX_X, ALU.max).then_inc(S["smx_done"], 1)
                else:
                    dve.wait_ge(S["sc_done"], b[1] + 1)
                    v.tensor_reduce(smx[:, 0:D], sc[:, par].rearrange("p t d -> p d t"), AX_X, ALU.max)\
                        .then_inc(S["smx_done"], 1)

            def diag_B(b):
                if not b or b[0] == MEAN:
                    return
                r = D if b[0] == CHAN else 1
                n = avg_item(*b)
                dve.wait_ge(S["mxt_done"], n)
                v.tensor_reduce(mcol[:], pj[0:D, 1, 0:P], AX_X, ALU.max).then_inc(S["mcol_done"], 1)
                v.tensor_scalar(diag[:, 0:D], ident[0:D, 0:D], pj[0:D, 0, 0:1], None, ALU.mult)
                dve.wait_ge(S["mcol_done"], n)
                v.tensor_scalar(diag[:, D:D + r], ident[0:D, 0:r], mcol[:], None, ALU.mult).then_inc(S["diag_done"], 1)

            def shift_B(b, par):
                if not b or b[0] == MEAN:
                    return
                dve.wait_ge(S["mbc_done"], avg_item(*b))
                if b[0] in ATT:
                    s1, s2 = hp[:, par, :, 0], hp[:, par, :, 1]
                    top_s = pj[:, 1, MAXIMA:MAXIMA + 1]
                    v.tensor_scalar(z08[:], s1, top_s, 1.0 - SLOPE, ALU.add, ALU.mult).then_inc(S["z08_done"], 1)
                    v.tensor_scalar(pre[:, 0], s2, top_s, 0.5, ALU.subtract, ALU.mult)
                    v.tensor_scalar(pre[:, 1], s2, top_s, SLOPE, ALU.subtract, ALU.mult)
                    dve.wait_ge(S["z08_done"], att_item(*b))
                    v.tensor_scalar(pre[:, 2], z08[:], 0.0, None, ALU.min)
                    v.tensor_scalar(pre[:, 3], z08[:], -1.0, 0.0, ALU.mult, ALU.min).then_inc(S["pre_done"], 1)
                else:
                    v.tensor_tensor(sc[:, par], sc[:, par], along(pj[:, 1, MAXIMA:MAXIMA + D]), ALU.subtract)\
                        .then_inc(S["scm_done"], 1)

            def hm_B(b, f, par):
                if not b or b[0] == MEAN:
                    return
                if f and f[0] != MEAN:
                    dve.wait_ge(S["filled_done"], avg_item(*f))
                v.tensor_copy(hm[:, par], pj[:, 1, MEANS:MEANS + D]).then_inc(S["hm_done"], 1)

            def cmp_B(b, par, j0, j1):
                if not b or b[0] not in ATT:
                    return
                for j in range(j0, j1):
                    dve.wait_ge(S["reach_done"], T * (att_item(*b) - 1) + j + 1)
                    v.tensor_tensor(C[:, par, j], reach[:, j], maskT[:, j], ALU.min).then_inc(S["c_done"], 1)

            def self_B(b, f, par):
                if not b or b[0] != MEAN:
                    return
                dve.wait_ge(S["hc_done"], b[1] + 1)
                if f and f[0] == MEAN:
                    dve.wait_ge(S["conv_done"], f[1] + 1)
                v.tensor_tensor(selfp[:, par], hc[:, par, :, 0:D], base[:], ALU.add).then_inc(S["self_done"], 1)

            def top_B(b, par):
                if not b or b[0] == MEAN:
                    return
                if b[0] in ATT:
                    n = att_item(*b)
                    dve.wait_ge(S["ex_done"], n)
                    v.scalar_tensor_tensor(out=vq[:, 0], in0=ex[:, par, 0], scalar=BIG, in1=ex[:, par, 0],
                                           op0=ALU.mult, op1=ALU.mult)
                    v.tensor_scalar(vq[:, 1], ex[:, par, 1], BIG, None, ALU.mult).then_inc(S["vq_done"], 1)
                    dve.wait_ge(S["vq_done"], n)
                    h1 = hp[:, par, :, 2:2 + V]
                    v.tensor_tensor(top[:, par, :, 0:V], h1, spread(vq[:, 0], V), ALU.mult)
                    v.tensor_tensor(top[:, par, :, V:VQ], h1, spread(vq[:, 1], V), ALU.mult).then_inc(S["top_done"], 1)
                else:
                    n = b[1] + 1
                    dve.wait_ge(S["ee_done"], n)
                    v.scalar_tensor_tensor(out=top[:, par, :, D:2 * D], in0=ee[:], scalar=BIG_E, in1=ee[:],
                                           op0=ALU.mult, op1=ALU.mult).then_inc(S["chE_done"], 1)
                    dve.wait_ge(S["chE_done"], n)
                    v.tensor_tensor(top[:, par, :, 0:D], top[:, par, :, D:2 * D], feat[:, par], ALU.mult)\
                        .then_inc(S["top_done"], 1)

            def rest_B(b, par):
                if not b:
                    return
                w = width[b[0]]
                if b[0] == MEAN:
                    dve.wait_ge(S["topcopy_done"], b[1] + 1)
                else:
                    dve.wait_ge(S["top_done"], avg_item(*b))
                v.tensor_tensor(rest[:, par, :, 0:w], top[:, par, :, 0:w], upper(top[:, par])[:, :, 0:w],
                                ALU.subtract).then_inc(S["rest_done"], 1)

            def low_B(b, par):
                if not b:
                    return
                w = width[b[0]]
                dve.wait_ge(S["rest_done"], item(*b))
                v.tensor_tensor(low[:, par, :, 0:w], rest[:, par, :, 0:w], upper(rest[:, par])[:, :, 0:w],
                                ALU.subtract).then_inc(S["low_done"], 1)

            def diff_F(f, par):
                if not f:
                    return
                dve.wait_ge(S["acc_free"], freed(*f, CH))
                if f[0] in ATT:
                    v.tensor_tensor(num[:, par, :, 0:V], num[:, par, :, 0:V], num[:, par, :, V:VQ], ALU.subtract)\
                        .then_inc(S["diff_done"], 1)
                if f[0] == MEAN:
                    v.tensor_tensor(conv[:], num[:, par, :, 0:D], selfp[:, par], ALU.add).then_inc(S["conv_done"], 1)

            def fill(f, par):
                v.copy_predicated(num[:, par, :, 0:D], spread(lone[:].bitcast(I32), D), along(hm[:, par]))\
                    .then_inc(S["filled_done"], 1)

            def rden_F(f, par):
                if not f:
                    return
                if f[0] in ATT:
                    n = att_item(*f)
                    dve.wait_ge(S["diff_done"], n)
                    v.tensor_tensor(den[:], num[:, par, :, D], lone[:], ALU.add).then_inc(S["den_done"], 1)
                    fill(f, par)
                    dve.wait_ge(S["den_done"], n)
                    v.reciprocal(rden[:, :, 0], den[:]).then_inc(S["rden_done"], 1)
                if f[0] == CHAN:
                    v.reciprocal(rden[:], num[:, par, :, D:2 * D]).then_inc(S["rden_done"], 1)
                    fill(f, par)
                if f[0] == MEAN:
                    dve.wait_ge(S["conv_relu_done"], f[1] + 1)
                    v.tensor_reduce(osum[:], sr[:], AX_X, ALU.add).then_inc(S["osum_done"], 1)

            def att_F(f, par):
                if not f:
                    return
                if f[0] != MEAN:
                    r = spread(rden[:, :, 0], D) if f[0] in ATT else rden[:]
                    dve.wait_ge(S["rden_done"], avg_item(*f))
                    dve.wait_ge(S["filled_done"], avg_item(*f))
                    v.tensor_tensor(att[:], num[:, par, :, 0:D], r, ALU.mult).then_inc(S["att_done"], 1)
                if f[0] == MEAN:
                    dve.wait_ge(S["osum_done"], f[1] + 1)
                    v.scalar_tensor_tensor(out=oc[:], in0=spread(osum[:], D), scalar=-1.0 / D, in1=sr[:],
                                           op0=ALU.mult, op1=ALU.add).then_inc(S["ocent_done"], 1)

            def ovar_F(f):
                if f and f[0] == MEAN:
                    dve.wait_ge(S["osq_done"], f[1] + 1)
                    v.tensor_reduce(ovar[:], osq[:], AX_X, ALU.add).then_inc(S["oss_done"], 1)
                    dve.wait_ge(S["oss_done"], f[1] + 1)
                    v.tensor_scalar(ovare[:], ovar[:], EPS, None, ALU.add).then_inc(S["ovar_done"], 1)

            def neg_F(f):
                if f and f[0] == ATT0:
                    dve.wait_ge(S["att_done"], avg_item(*f))
                    v.tensor_scalar(neg[:], att[:], 0.0, None, ALU.min).then_inc(S["neg_done"], 1)

            def scale_F(f):
                if f and f[0] == MEAN:
                    n = f[1] + 1
                    dve.wait_ge(S["orstd_done"], n)
                    v.tensor_tensor(oc[:], oc[:], spread(orstd[:], D), ALU.mult).then_inc(S["onorm_done"], 1)
                    dve.wait_ge(S["onorm_done"], n)
                    v.tensor_tensor(oc[:], oc[:], along(par_row(GAMMA)), ALU.mult).then_inc(S["ogamma_done"], 1)
                if f and f[0] == ATT0:
                    dve.wait_ge(S["en_done"], f[1] + 1)
                    v.scalar_tensor_tensor(out=so[:], in0=att[:], scalar=0.0, in1=en[:], op0=ALU.max, op1=ALU.add)\
                        .then_inc(S["elu_done"], 1)

            def beta_F(f):
                if f and f[0] == MEAN:
                    dve.wait_ge(S["ogamma_done"], f[1] + 1)
                    v.tensor_tensor(oc[:], oc[:], along(par_row(BETA)), ALU.add).then_inc(S["obeta_done"], 1)

            def x_F(f):
                if not f:
                    return
                l, b = f
                xb = x[:, b]
                if l == ATT0:
                    dve.wait_ge(S["elu_done"], b + 1)
                    v.scalar_tensor_tensor(out=xb, in0=so[:], scalar=-1.0, in1=xb, op0=ALU.add, op1=ALU.add)\
                        .then_inc(S["x_done"], 1)
                if l == MEAN:
                    dve.wait_ge(S["obeta_done"], b + 1)
                    v.tensor_tensor(xb, oc[:], xb, ALU.add).then_inc(S["x_done"], 1)
                if l == CHAN:
                    dve.wait_ge(S["att_done"], avg_item(l, b))
                    v.tensor_tensor(xb, att[:], xb, ALU.add).then_inc(S["x_done"], 1)
                if l == ATT3:
                    dve.wait_ge(S["att_done"], avg_item(l, b))
                    v.scalar_tensor_tensor(out=xb, in0=att[:], scalar=0.0, in1=xb, op0=ALU.max, op1=ALU.add)\
                        .then_inc(S["x_done"], 1)

            def step(a, b, m, f, half):
                other = 1 - half
                max_B(b, other)
                sum_A(a)
                diff_F(f, other)
                cent_A(a)
                cmp_B(b, other, 0, 1)
                rden_F(f, other)
                diag_B(b)
                cmp_B(b, other, 1, 2)
                att_F(f, other)
                var_A(a)
                cmp_B(b, other, 2, 3)
                shift_B(b, other)
                self_B(b, f, other)
                ovar_F(f)
                rest_B(b, other) if b and b[0] == MEAN else None
                neg_F(f)
                hm_B(b, f, other)
                cmp_B(b, other, 3, 4)
                h_A(a, half)
                scale_F(f)
                top_B(b, other)
                cmp_B(b, other, 4, 5)
                beta_F(f)
                if b and b[0] != MEAN:
                    rest_B(b, other)
                cmp_B(b, other, 5, 6)
                x_F(f)
                low_B(b, other)
                cmp_B(b, other, 6, T)
                feat_A(a, half)

            for g in range(2):
                dve.wait_ge(S["w_in"], W_IN)
                v.tensor_copy(arep[g][:], acol[g][:, 0:1].to_broadcast([D, P])).then_inc(S["arep_sb"], 1)
            for g in range(2):
                dve.wait_ge(S["wt_ps"], g + 1)
                v.tensor_copy(wtr[g][:], acc[0:D, g, 0:D]).then_inc(S["wt_sb"], 1)
            dve.wait_ge(S["const_g"], 1)
            sum_A((0, 0))
            cent_A((0, 0))
            for g in range(2):
                dve.wait_ge(S["wa_ps"], g + 1)
                for half in range(2):
                    q, o = slice(half * D, half * D + D), half * G
                    v.tensor_copy(wext[g][q, o:o + 2], acc[0:D, g, 128:130])
                    v.tensor_copy(w1rep[g][q], acc[0:D, g, 256:256 + P])
                    last = v.tensor_copy(wext[g][q, o + 2:o + G], wnat[g][:] if g == 0 else wtr[g][:])
                last.then_inc(S["wa_sb"], 1)
            var_A((0, 0))
            dve.wait_ge(S["rows_ps"], 1)
            v.tensor_copy(par_rows[:], acc[:, 2, 0:NR * D + 2]).then_inc(S["rows_sb"], 1)
            dve.wait_ge(S["rows_sb"], 1)
            v.tensor_scalar(k0[:], par_rows[:, NR * D:NR * D + 1], 0.7071067811865476, None, ALU.mult)
            v.tensor_copy(b0[:], par_rows[:, NR * D + 1:NR * D + 2]).then_inc(S["scal_sb"], 1)
            h_A((0, 0), 0)
            sum_A((0, 1))
            cent_A((0, 1))

            def mask_part(t):
                dve.wait_ge(S[f"adj_in{t}"], 16)
                v.tensor_scalar(mask[:, t], adj[:, t], 0.0, None, ALU.is_gt).then_inc(S["mask_nat"], 1)

            def maskT_part(t):
                dve.wait_ge(S["mask_tr"], t + 1)
                v.tensor_copy(maskT[:, :, t * P:(t + 1) * P],
                              acc[:, t % CH].bitcast(BF16).rearrange("p (j i) -> p j i", i=P)).then_inc(S["acc_free"], 1)

            mask_part(0)
            mask_part(1)
            var_A((0, 1))
            max_B((0, 0), 0)
            maskT_part(0)
            mask_part(2)
            diag_B((0, 0))
            h_A((0, 1), 1)
            maskT_part(1)
            mask_part(3)
            shift_B((0, 0), 0)
            hm_B((0, 0), None, 0)
            maskT_part(2)
            mask_part(4)
            top_B((0, 0), 0)
            maskT_part(3)
            mask_part(5)
            rest_B((0, 0), 0)
            maskT_part(4)
            mask_part(6)
            low_B((0, 0), 0)
            maskT_part(5)
            mask_part(7)
            maskT_part(6)
            maskT_part(7)
            dve.wait_ge(S["acc_free"], T)
            cmp_B((0, 0), 0, 0, T)
            dve.wait_ge(S["deg_sb"], T)
            for t in range(T):
                v.tensor_scalar(nmaskT[:, t], maskT[:, t], -1.0, None, ALU.mult).then_inc(S["nmask_sb"], 1)
            v.tensor_scalar(lone[:], deg[:], 0.0, None, ALU.is_equal)
            v.tensor_scalar(some[:], deg[:], 0.0, None, ALU.is_gt)
            v.tensor_scalar(deg1[:], deg[:], 1.0, None, ALU.max).then_inc(S["deg1_sb"], 1)
            dve.wait_ge(S["deg1_sb"], 1)
            v.reciprocal(rdeg[:], deg1[:])
            v.tensor_tensor(base[:], along(par_row(B_NEIGH)), spread(some[:], D), ALU.mult).then_inc(S["base_sb"], 1)
            dve.wait_ge(S["base_sb"], 1)
            v.tensor_tensor(base[:], base[:], along(par_row(B_SELF)), ALU.add).then_inc(S["base2_sb"], 1)
            dve.wait_ge(S["base2_sb"], 1)
            run(dve, step)

        @block.scalar
        def _(act):
            s = nc.scalar

            def sq_A(a):
                if a:
                    act.wait_ge(S["ln_cent"], item(*a))
                    s.activation(sq[:], cent[:], ACT.Square, scale=float(D) ** -0.5).then_inc(S["ln_sq"], 1)

            def hT_A(a):
                if a and a[0] != CHAN:
                    act.wait_ge(S["tr_done"], tr_item(*a))
                    s.activation(hT[:].rearrange("p k n -> p (k n)"), tp[:, 0], ACT.Copy).then_inc(S["hT_done"], 1)

            def hp_A(a, par):
                if not a or a[0] == CHAN:
                    return
                act.wait_ge(S["pj_done"], tr_item(*a))
                g, o = (2 * D, hc[:, par]) if a[0] == MEAN else (G, hp[:, par, :, 0:G])
                s.activation(o.rearrange("p (k t) g -> p k t g", k=2),
                             pj[:, :, 0:T // 2 * g].rearrange("p k (t g) -> p k t g", g=g), ACT.Copy)\
                    .then_inc(S["hc_done" if a[0] == MEAN else "hp_done"], 1)

            def s1_A(a):
                if a and a[0] in ATT:
                    if not very_first(a):
                        act.wait_ge(S["reach_done"], T * (att_item(*a) - 1))
                    act.wait_ge(S["s1_done"], att_item(*a))
                    s.activation(s1bc[:].rearrange("p (t k n) -> p k t n", k=2, n=P),
                                 tp[:].rearrange("p k (t n) -> p k t n", n=P), ACT.Copy).then_inc(S["s1bc_done"], 1)

            def soft_A(a, par):
                if not a or a[0] != CHAN:
                    return
                n = a[1] + 1
                act.wait_ge(S["h_done"], item(*a))
                s.activation(ab[:], h[:, par], ACT.Abs, scale=k0[:], bias=b0[:]).then_inc(S["ab_done"], 1)
                s.activation(rl[:], h[:, par], ACT.Relu, scale=k0[:], bias=b0[:]).then_inc(S["rl_done"], 1)
                act.wait_ge(S["ab_done"], n)
                s.activation(sp[:], ab[:], ACT.Exp, scale=-1.0).then_inc(S["e1_done"], 1)
                act.wait_ge(S["e1_done"], n)
                s.activation(sp[:], sp[:], ACT.Ln, bias=1.0).then_inc(S["ln1_done"], 1)

            def top_B(b, par):
                if b and b[0] == MEAN:
                    act.wait_ge(S["hc_done"], b[1] + 1)
                    s.activation(top[:, par, :, 0:D], hc[:, par, :, D:2 * D], ACT.Copy).then_inc(S["topcopy_done"], 1)

            def ex_B(b, par):
                if b and b[0] in ATT:
                    act.wait_ge(S["pre_done"], att_item(*b))
                    s.activation(ex[:, par], pre[:], ACT.Exp).then_inc(S["ex_done"], 1)

            def reach_B(b, par, j0, j1):
                if not b or b[0] not in ATT:
                    return
                n = att_item(*b)
                if j0 == 0:
                    act.wait_ge(S["s2big_done"], n)
                    act.wait_ge(S["s1bc_done"], n)
                for j in range(j0, j1):
                    s.activation(reach[:, j], s1bc[:], ACT.Relu, scale=BIG, bias=s2big[:, par, j:j + 1])\
                        .then_inc(S["reach_done"], 1)

            def ee_B(b, par):
                if b and b[0] == CHAN:
                    act.wait_ge(S["scm_done"], b[1] + 1)
                    s.activation(ee[:], sc[:, par], ACT.Exp, scale=0.5).then_inc(S["ee_done"], 1)

            def evac_M(m, par, c):
                if not m:
                    return
                l = m[0]
                act.wait_ge(S["main_done"], CH * (item(*m) - 1) + c + 1)
                for t in range(2 * c, 2 * c + 2):
                    o = t % 2 * VQ
                    if l in ATT:
                        s.activation(num[:, par, t, 0:V], acc[:, c, o:o + V], ACT.Copy, scale=ex[:, par, 2, t:t + 1])
                        last = s.activation(num[:, par, t, V:VQ], acc[:, c, o + V:o + VQ], ACT.Copy,
                                            scale=ex[:, par, 3, t:t + 1])
                    if l == MEAN:
                        last = s.activation(num[:, par, t, 0:D], acc[:, c, o:o + D], ACT.Copy, scale=rdeg[:, t:t + 1])
                    if l == CHAN:
                        s.activation(num[:, par, t, 0:D], acc[:, c, o:o + D], ACT.Copy)
                        last = s.activation(num[:, par, t, D:2 * D], acc[:, c, o + D:o + 2 * D], ACT.Identity,
                                            bias=lone[:, t:t + 1])
                last.then_inc(S["acc_free"], 1)

            def relu_F(f):
                if f and f[0] == MEAN:
                    act.wait_ge(S["conv_done"], f[1] + 1)
                    s.activation(sr[:], conv[:], ACT.Relu).then_inc(S["conv_relu_done"], 1)

            def sq_F(f):
                if f and f[0] == MEAN:
                    act.wait_ge(S["ocent_done"], f[1] + 1)
                    s.activation(osq[:], oc[:], ACT.Square, scale=float(D) ** -0.5).then_inc(S["osq_done"], 1)

            def elu_F(f):
                if f and f[0] == ATT0:
                    act.wait_ge(S["neg_done"], f[1] + 1)
                    s.activation(en[:], neg[:], ACT.Exp).then_inc(S["en_done"], 1)

            def step(a, b, m, f, half):
                other = 1 - half
                reach_B(b, other, 0, 1)
                top_B(b, other)
                relu_F(f)
                sq_A(a)
                reach_B(b, other, 1, 3)
                evac_M(m, half, 0)
                sq_F(f)
                ee_B(b, other)
                reach_B(b, other, 3, 4)
                ex_B(b, other)
                elu_F(f)
                evac_M(m, half, 1)
                reach_B(b, other, 4, 5)
                hT_A(a)
                reach_B(b, other, 5, 7)
                evac_M(m, half, 2)
                hp_A(a, half)
                reach_B(b, other, 7, T)
                s1_A(a)
                soft_A(a, half)
                evac_M(m, half, 3)

            def count(t):
                act.wait_ge(S["mask_nat"], t + 1)
                if t:
                    act.wait_ge(S["deg_sb"], t)
                s.activation(count_bin, mask[:, t], ACT.Copy, accum_out=deg[:, t:t + 1]).then_inc(S["deg_sb"], 1)

            av = adj_in.rearrange("(p t) n -> p t n", t=T)
            for t in range(T):
                act.dma_start(adj[:, t], av[:, t]).then_inc(S[f"adj_in{t}"], 16)
            sq_A((0, 0))
            hT_A((0, 0))
            hp_A((0, 0), 0)
            sq_A((0, 1))
            s1_A((0, 0))
            count(0)
            count(1)
            reach_B((0, 0), 0, 0, 1)
            ex_B((0, 0), 0)
            hT_A((0, 1))
            count(2)
            reach_B((0, 0), 0, 1, 3)
            hp_A((0, 1), 1)
            count(3)
            reach_B((0, 0), 0, 3, T)
            s1_A((0, 1))
            for t in range(4, T):
                count(t)
            run(act, step)

        @block.tensor
        def _(pe):
            mm = nc.tensor.matmul

            def tr_A(a, par):
                if not a or a[0] == CHAN:
                    return
                if not very_first(a):
                    pe.wait_ge(S["s1bc_done"], B if a[0] == MEAN else att_item(*a) - 1)
                pe.wait_ge(S["h_done"], item(*a))
                for t in range(T // 2):
                    last = nc.tensor.transpose(tp[:, 0, t * P:(t + 1) * P],
                                               h[:, par, 2 * t:2 * t + 2].rearrange("p t d -> p (t d)"), ident[:])
                last.then_inc(S["tr_done"], 1)

            def proj_A(a, b):
                if not a or a[0] == CHAN:
                    return
                if b and b[0] != MEAN:
                    pe.wait_ge(S["hm_done"], avg_item(*b))
                if b and b[0] == MEAN:
                    pe.wait_ge(S["hc_done"], b[1] + 1)
                w = wconv if a[0] == MEAN else wext[a[0] // 3]
                g = 4 * D if a[0] == MEAN else 2 * G
                pe.wait_ge(S["hT_done"], tr_item(*a))
                for t in range(T // 2):
                    o = t % 2 * g
                    last = mm(pj[:, t // 2, o:o + g], hT[:, t], w[:, 0:g], start=True, stop=True)
                last.then_inc(S["pj_done"], 1)

            def s1_A(a):
                if a and a[0] in ATT:
                    for k in range(2):
                        q = slice(k * D, k * D + D)
                        last = mm(tp[:, k], w1rep[a[0] // 3][q], hT[q].rearrange("p t n -> p (t n)"), start=True, stop=True)
                    last.then_inc(S["s1_done"], 1)

            def mxt_B(b, par):
                if not b or b[0] == MEAN:
                    return
                pe.wait_ge(S["smx_done"], avg_item(*b))
                nc.tensor.transpose(pj[:, 1, 0:P], smx[:], ident[:])
                for t in range(T):
                    r = feat[:, par, t] if b[0] == CHAN else hp[:, par, t, 2:2 + D]
                    last = mm(pj[0:D, 0, 0:1], r, avg[:], start=(t == 0), stop=(t == T - 1))
                last.then_inc(S["mxt_done"], 1)

            def mbc_B(b):
                if not b or b[0] == MEAN:
                    return
                r = D + (D if b[0] == CHAN else 1)
                pe.wait_ge(S["diag_done"], avg_item(*b))
                mm(pj[:, 1, MEANS:MEANS + r], ones[0:D], diag[:, 0:r], start=True, stop=True).then_inc(S["mbc_done"], 1)

            def main_M(m, par, i):
                if not m:
                    return
                l = m[0]
                c, w, o = i // 2, width[l], i % 2 * VQ
                if i == 0:
                    pe.wait_ge(S["low_done"], item(*m))
                if i % 2 == 0:
                    pe.wait_ge(S["acc_free"], freed(*m, c + 1 - CH))
                cuts = (upper(top[:, par]), upper(rest[:, par]), low[:, par])
                rowt = slice(i * P, (i + 1) * P)
                lhs = C[:, par] if l in ATT else maskT[:]
                for j in range(T):
                    if i == 0 and l in ATT:
                        pe.wait_ge(S["c_done"], T * (att_item(*m) - 1) + j + 1)
                    for s_ in range(3):
                        last = mm(acc[:, c, o:o + w], lhs[:, j, rowt], cuts[s_][:, j, 0:w], start=(j == 0 and s_ == 0),
                                  stop=(l not in ATT and j == T - 1 and s_ == 2))
                if l in ATT:
                    if very_first(m) and i == 0:
                        pe.wait_ge(S["nmask_sb"], T)
                    for j in range(T):
                        for s_ in range(3):
                            last = mm(acc[:, c, o + V:o + VQ], nmaskT[:, j, rowt], cuts[s_][:, j, V:VQ],
                                      start=False, stop=(j == T - 1 and s_ == 2))
                if i % 2 == 1:
                    last.then_inc(S["main_done"], 1)

            def step(a, b, m, f, half):
                other = 1 - half
                wide = m and m[0] in ATT
                main_M(m, half, 0)
                main_M(m, half, 1)
                if wide:
                    mxt_B(b, other)
                main_M(m, half, 2)
                if wide:
                    mbc_B(b)
                main_M(m, half, 3)
                if not wide:
                    mxt_B(b, other)
                main_M(m, half, 4)
                if wide:
                    tr_A(a, half)
                main_M(m, half, 5)
                if not wide:
                    mbc_B(b)
                if wide:
                    proj_A(a, b)
                main_M(m, half, 6)
                if wide:
                    s1_A(a)
                main_M(m, half, 7)
                if not wide:
                    tr_A(a, half)
                    proj_A(a, b)
                    s1_A(a)

            pe.wait_ge(S["identb_g"], 1)
            pe.wait_ge(S["w_in"], W_IN)
            for g in range(2):
                nc.tensor.transpose(acc[0:D, g, 0:D], wnat[g][:], ident[0:D, 0:D]).then_inc(S["wt_ps"], 1)
            mm(acc[:, 2, 0:NR * D + 2], ones[0:1, :], rows[:], start=True, stop=True).then_inc(S["rows_ps"], 1)
            pe.wait_ge(S["arep_sb"], 2)
            for g in range(2):
                pe.wait_ge(S["wt_sb"], g + 1)
                w = wtr[g] if g == 0 else wnat[g]
                mm(acc[0:D, g, 128:130], w[:], acol[g][:], start=True, stop=True)
                mm(acc[0:D, g, 256:256 + P], w[:], arep[g][:], start=True, stop=True).then_inc(S["wa_ps"], 1)
            pe.wait_ge(S["wa_sb"], 2)

            def mask_tr(t):
                pe.wait_ge(S["mask_nat"], t + 1)
                if t == 0:
                    pe.wait_ge(S["scal_sb"], 1)
                if t >= CH:
                    pe.wait_ge(S["acc_free"], t - CH + 1)
                for j in range(T):
                    last = nc.tensor.transpose(acc[:, t % CH].bitcast(BF16)[:, j * P:(j + 1) * P],
                                               mask[:, t].rearrange("p (q j) -> p j q", j=T)[:, j], identb[:])
                last.then_inc(S["mask_tr"], 1)

            tr_A((0, 0), 0)
            proj_A((0, 0), None)
            s1_A((0, 0))
            mask_tr(0)
            mxt_B((0, 0), 0)
            mask_tr(1)
            mbc_B((0, 0))
            mask_tr(2)
            mask_tr(3)
            tr_A((0, 1), 1)
            mask_tr(4)
            proj_A((0, 1), (0, 0))
            mask_tr(5)
            s1_A((0, 1))
            mask_tr(6)
            mask_tr(7)
            run(pe, step)


_WEIGHTS = ['L0_gnn_W', 'L0_gnn_a', 'L1_gnn_W_self', 'L1_gnn_b_self', 'L1_gnn_W_neigh', 'L1_gnn_b_neigh',
            'L1_gnn_ln_gamma', 'L1_gnn_ln_beta', 'L2_gnn_w0', 'L2_gnn_b0', 'L2_gnn_wa', 'L2_gnn_ba',
            'L3_gnn_W', 'L3_gnn_a']


def kernel(**inputs):
    import numpy as _np
    import concourse.bacc as _bacc
    from concourse import mybir as _mybir
    from concourse.bass_utils import run_bass_kernel_spmd as _run

    nc = _bacc.Bacc("TRN2", target_bir_lowering=False, num_devices=1)
    arrays, aps = {}, {}
    for name in ['x', 'adj'] + _WEIGHTS:
        a = _np.ascontiguousarray(inputs[name])
        arrays[f"in_{name}"] = a
        aps[name] = nc.dram_tensor(f"in_{name}", a.shape, _mybir.dt.from_np(a.dtype), kind="ExternalInput").ap()
    o = nc.dram_tensor("out_x", inputs['x'].shape, _mybir.dt.float32, kind="ExternalOutput").ap()
    build(nc, aps['x'], aps['adj'], {n: aps[n] for n in _WEIGHTS}, o)
    r = _run(nc, [arrays], core_ids=[0])
    return r.results[0]["out_x"]
```

```python
from contextlib import ExitStack

import concourse.bass as bass
from concourse import mybir

ALU = mybir.AluOpType
ACT = mybir.ActivationFunctionType
F32 = mybir.dt.float32
BF16 = mybir.dt.bfloat16
I32 = mybir.dt.int32
AX_X = mybir.AxisListType.X


P = 128
ATT0, MEAN, CHAN, ATT3 = range(4)
LAYERS = 4
EPS = 1e-5
SLOPE = 0.2
BIG = float(2.0 ** 100)
BIG_E = float(2.0 ** 80)


def build(nc, x_in, adj_in, w_in, out):
    B, N, D = x_in.shape
    T = N // P
    G = D + 2
    V = D + 1
    VQ = 2 * V
    CH = T // 2
    SPLIT = 3
    NR = 6

    with ExitStack() as ctx:
        def sb(name, shape, dt=F32):
            return ctx.enter_context(nc.sbuf_tensor(name, shape, dt))

        def ps(name, shape):
            return ctx.enter_context(nc.psum_tensor(name, shape, F32))

        def sem(name):
            return ctx.enter_context(nc.semaphore(name))

        x = sb("x", [P, B, T, D])
        maskT = sb("maskT", [P, T, N], BF16)
        nmaskT = sb("nmaskT", [P, T, N], BF16)
        deg = sb("deg", [P, T])
        deg1 = sb("deg1", [P, T])
        rdeg = sb("rdeg", [P, T])
        lone = sb("lone", [P, T])
        some = sb("some", [P, T])
        base = sb("base", [P, T, D])
        ones = sb("ones", [P, P])
        ident = sb("ident", [P, P])
        identb = sb("identb", [P, P], BF16)
        onesb = sb("onesb", [P, 1], BF16)
        avg = sb("avg", [P, 1])
        mhalf = sb("mhalf", [P, T])
        mone = sb("mone", [P, 1])
        rows = sb("rows", [1, NR * D + 2])
        par_rows = sb("par_rows", [P, NR * D + 2])
        k0 = sb("k0", [P, 1])
        b0 = sb("b0", [P, 1])
        wnat = [sb(f"wnat{g}", [D, D]) for g in range(2)]
        wtr = [sb(f"wtr{g}", [D, D]) for g in range(2)]
        acol = [sb(f"acol{g}", [D, 2]) for g in range(2)]
        arep = [sb(f"arep{g}", [D, P]) for g in range(2)]
        wext = [sb(f"wext{g}", [P, 2 * G]) for g in range(2)]
        wconv = sb("wconv", [P, 4 * D])
        wstack = [sb(f"wstack{g}", [P, D]) for g in range(2)]
        w1rep = [sb(f"w1rep{g}", [P, P]) for g in range(2)]
        lnsum = sb("lnsum", [P, T])
        cent = sb("cent", [P, T, D])
        sq = sb("sq", [P, T, D])
        var = sb("var", [P, T])
        vare = sb("vare", [P, T])
        rstd = sb("rstd", [P, T])
        h = sb("h", [P, 2, T, D])
        hT = sb("hT", [P, T // 2, P])
        hp = sb("hp", [P, 2, T, G + 2])
        s1bc = sb("s1bc", [P, N])
        hc = sb("hc", [P, 2, T, 2 * D])
        ab = sb("ab", [P, T, D])
        soft = sb("soft", [P, 2, T, D])
        rl, sp = soft[:, 0], soft[:, 1]
        feat = sb("feat", [P, 2, T, D])
        sc = sb("sc", [P, 2, T, D])
        selfp = sb("selfp", [P, 2, T, D])
        smx = sb("smx", [P, P])
        mcol = sb("mcol", [D, 1])
        diag = sb("diag", [D, 2 * D])
        hsum = sb("hsum", [P, 2])
        hm = sb("hm", [P, 2, D])
        s2big = sb("s2big", [P, 2, T])
        z08 = sb("z08", [P, T])
        pre = sb("pre", [P, 4, T])
        ex = sb("ex", [P, 2, 4, T])
        vq = sb("vq", [P, 2, T])
        ee = sb("ee", [P, T, D])
        reach = sb("reach", [P, T, N], BF16)
        C = sb("C", [P, 2, T, N], BF16)
        miss = sb("miss", [P, SPLIT - 1, 2, N], BF16)
        adj = C[:].rearrange("p a t n -> p (a t n)").bitcast(I32).rearrange("p (t n) -> p t n", t=T)
        mask = nmaskT
        last_miss = soft[:].rearrange("p a t d -> p a (t d)").bitcast(BF16)

        def miss_tile(par, j):
            return miss[:, j, par] if j < SPLIT - 1 else last_miss[:, par]
        top = sb("top", [P, 2, T, VQ])
        rest = sb("rest", [P, 2, T, VQ])
        low = sb("low", [P, 2, T, VQ], BF16)
        num = sb("num", [P, 2, T, VQ])
        den = sb("den", [P, T])
        rden = sb("rden", [P, T, D])
        att = sb("att", [P, T, D])
        em1 = sb("em1", [P, T, D])
        en = sb("en", [P, T, D])
        so = sb("so", [P, T, D])
        conv = sb("conv", [P, T, D])
        sr = sb("sr", [P, T, D])
        osum = sb("osum", [P, T])
        ovar = sb("ovar", [P, T])
        ovare = sb("ovare", [P, T])
        orstd = sb("orstd", [P, T])
        oc, osq = em1, en

        acc = ps("acc", [P, CH, 512])
        tp = ps("tp", [P, 2, 512])
        pj = ps("pj", [P, 2, 512])
        MEANS = P
        MAXIMA = P + D
        DEG = 2 * VQ

        def mask_bank(t):
            return acc[:, t % CH].bitcast(BF16).rearrange("p (j i) -> p j i", i=P)

        names = """x_in0 x_in1 x_in2 w_in row_in const_g ident_g identb_g rows_ps rows_sb wt_ps wt_sb arep_sb wa_ps wa_sb
            mask_nat mask_tr maskT_dve maskT_act acc_free nmask_dve nmask_act deg_ps deg_sb deg1_sb base_sb base2_sb
            ln_sum ln_cent ln_sq ln_ss ln_var ln_rstd h_done tr_done hT_done pj_done s1_done hp_done s1bc_done hc_done
            ab_done e1_done ln1_done feat_done sc1_done sc_done
            smx_done mxt_done mcol_done diag_done mbc_done hm_done s2big_done z08_done pre_done ex_done
            vq_done reach_done c_done miss_done scm_done ee_done chE_done topcopy_done top_done rest_done low_done main_done
            diff_done den_done rden_done att_done filled_done pos_done en_done em1_done
            conv_done conv_relu_done osum_done ocent_done osq_done oss_done ovar_done orstd_done
            onorm_done ogamma_done obeta_done x_done out_done""".split() + [f"adj_in{k}" for k in range(T // 2)]
        S = {n: sem(n) for n in names}

        def item(l, b):
            return B * l + b + 1

        def att_item(l, b):
            return B * (l // 3) + b + 1

        def avg_item(l, b):
            return B * (0, 0, 1, 2)[l] + b + 1

        def tr_item(l, b):
            return B * (0, 1, 1, 2)[l] + b + 1

        def freed(l, b, c):
            return CH * (item(l, b) - 1) + c

        def upper(t):
            return t.bitcast(BF16).rearrange("p t (v two) -> p t v two", two=2)[:, :, :, 1]

        def spread(t, d):
            return t.unsqueeze(2).to_broadcast([P, t.shape[1], d])

        def along(r):
            return r.unsqueeze(1).to_broadcast([P, T, r.shape[1]])

        width = (VQ, D, 2 * D, VQ)
        ATT = (ATT0, ATT3)

        def very_first(it):
            return isinstance(it[1], int) and it == (0, 0)

        def par_row(n):
            return par_rows[:, n * D:(n + 1) * D]

        B_SELF, B_NEIGH, GAMMA, BETA, WA, BA = range(NR)

        def run(eng, step):
            for l in range(LAYERS):
                def nxt(b):
                    return (l + 1, b) if l + 1 < LAYERS else None
                step((l, 2), (l, 1), (l, 0), (l - 1, B - 1) if l else None, 0)
                step((l, 3), (l, 2), (l, 1), (l, 0), 1)
                with eng.Fori(2, B - 3, 2) as b:
                    step((l, b + 2), (l, b + 1), (l, b), (l, b - 1), 0)
                    step((l, b + 3), (l, b + 2), (l, b + 1), (l, b), 1)
                step(nxt(0), (l, B - 1), (l, B - 2), (l, B - 3), 0)
                step(nxt(1), nxt(0), (l, B - 1), (l, B - 2), 1)
            step(None, None, None, (LAYERS - 1, B - 1), 0)

        block = ctx.enter_context(nc.Block())

        @block.sync
        def _(sync):
            xv = x_in.rearrange("b (p t) d -> p b (t d)", t=T)
            xs = x[:].rearrange("p b t d -> p b (t d)")
            sync.dma_start(xs[:, 0:1], xv[:, 0:1]).then_inc(S["x_in0"], 16)
            sync.dma_start(xs[:, 1:2], xv[:, 1:2]).then_inc(S["x_in1"], 16)
            for n, name in enumerate(("L1_gnn_b_self", "L1_gnn_b_neigh", "L1_gnn_ln_gamma", "L1_gnn_ln_beta",
                                      "L2_gnn_wa", "L2_gnn_ba")):
                sync.dma_start(rows[0:1, n * D:(n + 1) * D], w_in[name].rearrange("(o d) -> o d", o=1)).then_inc(S["row_in"], 16)
            sync.dma_start(rows[0:1, NR * D:NR * D + 1], w_in["L2_gnn_w0"]).then_inc(S["row_in"], 16)
            sync.dma_start(rows[0:1, NR * D + 1:NR * D + 2],
                           w_in["L2_gnn_b0"].rearrange("(o d) -> o d", o=1)).then_inc(S["row_in"], 16)
            sync.wait_ge(S["const_g"], 1)
            for half in range(2):
                q, o = slice(half * D, half * D + D), half * 2 * D
                sync.dma_start(wconv[q, o:o + D], w_in["L1_gnn_W_self"]).then_inc(S["row_in"], 16)
                sync.dma_start(wconv[q, o + D:o + 2 * D], w_in["L1_gnn_W_neigh"]).then_inc(S["row_in"], 16)
            sync.dma_start(xs[:, 2:B], xv[:, 2:B]).then_inc(S["x_in2"], 16)
            ov = out.rearrange("b (p t) d -> p b (t d)", t=T)
            for b in range(B):
                sync.wait_ge(S["x_done"], item(ATT3, b))
                sync.dma_start(ov[:, b:b + 1], xs[:, b:b + 1]).then_inc(S["out_done"], 16)
            sync.wait_ge(S["out_done"], 16 * B)
        W_IN, ROW_IN = 16 * 6, 16 * 12

        @block.gpsimd
        def _(pool):
            g = nc.gpsimd
            g.memset(ones[:], 1.0)
            g.memset(onesb[:], 1.0)
            g.memset(avg[:], 1.0 / N)
            g.memset(mhalf[:], -0.5)
            g.memset(mone[:], -1.0)
            g.memset(smx[:], 0.0)
            g.memset(wext[0][:], 0.0)
            g.memset(wext[1][:], 0.0)
            g.memset(wconv[:], 0.0)
            g.memset(hp[:, :, :, G:G + 1], 1.0)
            g.memset(ident[:], 0.0).then_inc(S["const_g"], 1)
            pool.wait_ge(S["const_g"], 1)
            g.affine_select(out=ident[:], in_=ident[:], compare_op=ALU.not_equal, fill=1.0, base=0,
                            pattern=[[-1, P]], channel_multiplier=1).then_inc(S["ident_g"], 1)
            pool.wait_ge(S["ident_g"], 1)
            g.tensor_copy(identb[:], ident[:]).then_inc(S["identb_g"], 1)

            def rstd_A(a):
                if not a:
                    return
                pool.wait_ge(S["ln_var"], item(*a))
                g.tensor_tensor(rstd[:], vare[:], mhalf[:], ALU.pow).then_inc(S["ln_rstd"], 1)

            def rstd_F(f):
                if not f or f[0] != MEAN:
                    return
                pool.wait_ge(S["ovar_done"], f[1] + 1)
                g.tensor_tensor(orstd[:], ovare[:], mhalf[:], ALU.pow).then_inc(S["orstd_done"], 1)

            def step(a, b, m, f, half):
                rstd_A(a)
                rstd_F(f)

            rstd_A((0, 0))
            rstd_A((0, 1))
            run(pool, step)

        @block.vector
        def _(dve):
            v = nc.vector

            def sum_A(a):
                if not a:
                    return
                l, b = a
                if l == 0:
                    dve.wait_ge(S[f"x_in{b}" if isinstance(b, int) and b < 2 else "x_in2"], 16)
                else:
                    dve.wait_ge(S["x_done"], item(l - 1, b))
                v.tensor_reduce(lnsum[:], x[:, b], AX_X, ALU.add).then_inc(S["ln_sum"], 1)

            def cent_A(a):
                if not a:
                    return
                dve.wait_ge(S["ln_sum"], item(*a))
                v.scalar_tensor_tensor(out=cent[:], in0=spread(lnsum[:], D), scalar=-1.0 / D, in1=x[:, a[1]],
                                       op0=ALU.mult, op1=ALU.add).then_inc(S["ln_cent"], 1)

            def var_A(a):
                if not a:
                    return
                dve.wait_ge(S["ln_sq"], item(*a))
                v.tensor_reduce(var[:], sq[:], AX_X, ALU.add).then_inc(S["ln_ss"], 1)
                dve.wait_ge(S["ln_ss"], item(*a))
                v.tensor_scalar(vare[:], var[:], EPS, None, ALU.add).then_inc(S["ln_var"], 1)

            def h_A(a, par):
                if not a:
                    return
                dve.wait_ge(S["ln_rstd"], item(*a))
                v.scalar_tensor_tensor(out=h[:, par], in0=cent[:], scalar=0.0, in1=spread(rstd[:], D),
                                       op0=ALU.max, op1=ALU.mult).then_inc(S["h_done"], 1)

            def feat_A(a, par):
                if not a or a[0] != CHAN:
                    return
                n = a[1] + 1
                dve.wait_ge(S["ln1_done"], n)
                v.tensor_tensor(feat[:, par], rl, sp, ALU.add).then_inc(S["feat_done"], 1)
                dve.wait_ge(S["feat_done"], n)
                v.tensor_tensor(sc[:, par], feat[:, par], along(par_row(WA)), ALU.mult).then_inc(S["sc1_done"], 1)
                dve.wait_ge(S["sc1_done"], n)
                v.tensor_tensor(sc[:, par], sc[:, par], along(par_row(BA)), ALU.add).then_inc(S["sc_done"], 1)

            def max_B(b, par):
                if not b or b[0] == MEAN:
                    return
                if b[0] in ATT:
                    s2 = hp[:, par, :, 1]
                    dve.wait_ge(S["hp_done"], att_item(*b))
                    v.tensor_scalar(s2big[:, par], s2, BIG, None, ALU.mult).then_inc(S["s2big_done"], 1)
                    v.tensor_reduce(smx[:, 0:1], s2, AX_X, ALU.max).then_inc(S["smx_done"], 1)
                else:
                    dve.wait_ge(S["sc_done"], b[1] + 1)
                    v.tensor_reduce(smx[:, 0:D], sc[:, par].rearrange("p t d -> p d t"), AX_X, ALU.max)\
                        .then_inc(S["smx_done"], 1)

            def diag_B(b):
                if not b or b[0] == MEAN:
                    return
                r = D if b[0] == CHAN else 1
                n = avg_item(*b)
                dve.wait_ge(S["mxt_done"], n)
                v.tensor_reduce(mcol[0:r], pj[0:r, 1, 0:P], AX_X, ALU.max).then_inc(S["mcol_done"], 1)
                if b[0] == CHAN:
                    v.tensor_scalar(diag[:, 0:D], ident[0:D, 0:D], pj[0:D, 0, 0:1], None, ALU.mult)
                    dve.wait_ge(S["mcol_done"], n)
                    v.tensor_scalar(diag[:, D:2 * D], ident[0:D, 0:D], mcol[:], None, ALU.mult).then_inc(S["diag_done"], 1)

            def shift_B(b, par):
                if not b or b[0] == MEAN:
                    return
                dve.wait_ge(S["mbc_done"], avg_item(*b))
                if b[0] in ATT:
                    s1, s2 = hp[:, par, :, 0], hp[:, par, :, 1]
                    top_s = pj[:, 1, MAXIMA:MAXIMA + 1]
                    v.tensor_scalar(z08[:], s1, top_s, 1.0 - SLOPE, ALU.add, ALU.mult).then_inc(S["z08_done"], 1)
                    v.tensor_scalar(pre[:, 0], s2, top_s, 0.5, ALU.subtract, ALU.mult)
                    v.tensor_scalar(pre[:, 1], s2, top_s, SLOPE, ALU.subtract, ALU.mult)
                    dve.wait_ge(S["z08_done"], att_item(*b))
                    v.tensor_scalar(pre[:, 2], z08[:], 0.0, None, ALU.min)
                    v.tensor_scalar(pre[:, 3], z08[:], -1.0, 0.0, ALU.mult, ALU.min).then_inc(S["pre_done"], 1)
                else:
                    v.tensor_tensor(sc[:, par], sc[:, par], along(pj[:, 1, MAXIMA:MAXIMA + D]), ALU.subtract)\
                        .then_inc(S["scm_done"], 1)

            def hm_B(b, f, par):
                if not b or b[0] == MEAN:
                    return
                if f and f[0] != MEAN:
                    dve.wait_ge(S["filled_done"], avg_item(*f))
                scale = 1.0 / N if b[0] in ATT else 1.0
                v.tensor_scalar(hm[:, par], pj[:, 1, MEANS:MEANS + D], scale, None, ALU.mult).then_inc(S["hm_done"], 1)

            def cmp_B(b, par, j0, j1):
                if not b or b[0] not in ATT:
                    return
                for j in range(j0, j1):
                    dve.wait_ge(S["reach_done"], T * (att_item(*b) - 1) + j + 1)
                    v.tensor_tensor(C[:, par, j], reach[:, j], maskT[:, j], ALU.min).then_inc(S["c_done"], 1)

            def miss_B(b, par, j):
                if not b or b[0] not in ATT:
                    return
                dve.wait_ge(S["c_done"], T * (att_item(*b) - 1) + j + 1)
                v.tensor_tensor(miss_tile(par, j), C[:, par, j], nmaskT[:, j], ALU.add).then_inc(S["miss_done"], 1)

            def self_B(b, f, par):
                if not b or b[0] != MEAN:
                    return
                dve.wait_ge(S["hc_done"], b[1] + 1)
                if f and f[0] == MEAN:
                    dve.wait_ge(S["conv_done"], f[1] + 1)
                v.tensor_tensor(selfp[:, par], hc[:, par, :, 0:D], base[:], ALU.add)

            def top_B(b, par):
                if not b or b[0] == MEAN:
                    return
                if b[0] in ATT:
                    n = att_item(*b)
                    dve.wait_ge(S["ex_done"], n)
                    v.scalar_tensor_tensor(out=vq[:, 0], in0=ex[:, par, 0], scalar=BIG, in1=ex[:, par, 0],
                                           op0=ALU.mult, op1=ALU.mult)
                    v.tensor_scalar(vq[:, 1], ex[:, par, 1], BIG, None, ALU.mult).then_inc(S["vq_done"], 1)
                    dve.wait_ge(S["vq_done"], n)
                    h1 = hp[:, par, :, 2:2 + V]
                    v.tensor_tensor(top[:, par, :, 0:V], h1, spread(vq[:, 0], V), ALU.mult)
                    v.tensor_tensor(top[:, par, :, V:VQ], h1, spread(vq[:, 1], V), ALU.mult).then_inc(S["top_done"], 1)
                else:
                    dve.wait_ge(S["chE_done"], b[1] + 1)
                    v.tensor_tensor(top[:, par, :, 0:D], top[:, par, :, D:2 * D], feat[:, par], ALU.mult)\
                        .then_inc(S["top_done"], 1)

            def rest_B(b, par):
                if not b:
                    return
                w = width[b[0]]
                if b[0] == MEAN:
                    dve.wait_ge(S["topcopy_done"], b[1] + 1)
                else:
                    dve.wait_ge(S["top_done"], avg_item(*b))
                v.tensor_tensor(rest[:, par, :, 0:w], top[:, par, :, 0:w], upper(top[:, par])[:, :, 0:w],
                                ALU.subtract).then_inc(S["rest_done"], 1)

            def low_B(b, par):
                if not b:
                    return
                w = width[b[0]]
                dve.wait_ge(S["rest_done"], item(*b))
                v.tensor_tensor(low[:, par, :, 0:w], rest[:, par, :, 0:w], upper(rest[:, par])[:, :, 0:w],
                                ALU.subtract).then_inc(S["low_done"], 1)

            def diff_F(f, par):
                if not f:
                    return
                dve.wait_ge(S["acc_free"], freed(*f, CH))
                if f[0] in ATT:
                    v.tensor_tensor(num[:, par, :, 0:V], num[:, par, :, 0:V], num[:, par, :, V:VQ], ALU.subtract)\
                        .then_inc(S["diff_done"], 1)
                if f[0] == MEAN:
                    v.tensor_tensor(conv[:], num[:, par, :, 0:D], selfp[:, par], ALU.add).then_inc(S["conv_done"], 1)

            def fill(f, par):
                v.copy_predicated(num[:, par, :, 0:D], spread(lone[:].bitcast(I32), D), along(hm[:, par]))\
                    .then_inc(S["filled_done"], 1)

            def rden_F(f, par):
                if not f:
                    return
                if f[0] in ATT:
                    n = att_item(*f)
                    dve.wait_ge(S["diff_done"], n)
                    v.tensor_tensor(den[:], num[:, par, :, D], lone[:], ALU.add).then_inc(S["den_done"], 1)
                    fill(f, par)
                    dve.wait_ge(S["den_done"], n)
                    v.reciprocal(rden[:, :, 0], den[:]).then_inc(S["rden_done"], 1)
                if f[0] == CHAN:
                    v.reciprocal(rden[:], num[:, par, :, D:2 * D]).then_inc(S["rden_done"], 1)
                if f[0] == MEAN:
                    dve.wait_ge(S["conv_relu_done"], f[1] + 1)
                    v.tensor_reduce(osum[:], sr[:], AX_X, ALU.add).then_inc(S["osum_done"], 1)

            def att_F(f, par):
                if not f:
                    return
                if f[0] != MEAN:
                    r = spread(rden[:, :, 0], D) if f[0] in ATT else rden[:]
                    dve.wait_ge(S["rden_done"], avg_item(*f))
                    dve.wait_ge(S["filled_done"], avg_item(*f))
                    v.tensor_tensor(att[:], num[:, par, :, 0:D], r, ALU.mult).then_inc(S["att_done"], 1)
                if f[0] == MEAN:
                    dve.wait_ge(S["osum_done"], f[1] + 1)
                    v.scalar_tensor_tensor(out=oc[:], in0=spread(osum[:], D), scalar=-1.0 / D, in1=sr[:],
                                           op0=ALU.mult, op1=ALU.add).then_inc(S["ocent_done"], 1)

            def ovar_F(f):
                if f and f[0] == MEAN:
                    dve.wait_ge(S["osq_done"], f[1] + 1)
                    v.tensor_reduce(ovar[:], osq[:], AX_X, ALU.add).then_inc(S["oss_done"], 1)
                    dve.wait_ge(S["oss_done"], f[1] + 1)
                    v.tensor_scalar(ovare[:], ovar[:], EPS, None, ALU.add).then_inc(S["ovar_done"], 1)

            def pos_F(f):
                if f and f[0] == ATT0:
                    dve.wait_ge(S["att_done"], avg_item(*f))
                    v.scalar_tensor_tensor(out=so[:], in0=att[:], scalar=0.0, in1=x[:, f[1]], op0=ALU.max, op1=ALU.add)\
                        .then_inc(S["pos_done"], 1)

            def scale_F(f):
                if f and f[0] == MEAN:
                    n = f[1] + 1
                    dve.wait_ge(S["orstd_done"], n)
                    v.tensor_tensor(oc[:], oc[:], spread(orstd[:], D), ALU.mult).then_inc(S["onorm_done"], 1)
                    dve.wait_ge(S["onorm_done"], n)
                    v.tensor_tensor(oc[:], oc[:], along(par_row(GAMMA)), ALU.mult).then_inc(S["ogamma_done"], 1)

            def beta_F(f):
                if f and f[0] == MEAN:
                    dve.wait_ge(S["ogamma_done"], f[1] + 1)
                    v.tensor_tensor(oc[:], oc[:], along(par_row(BETA)), ALU.add).then_inc(S["obeta_done"], 1)

            def x_F(f):
                if not f:
                    return
                l, b = f
                xb = x[:, b]
                if l == ATT0:
                    dve.wait_ge(S["pos_done"], b + 1)
                    dve.wait_ge(S["em1_done"], b + 1)
                    v.scalar_tensor_tensor(out=xb, in0=em1[:], scalar=0.0, in1=so[:], op0=ALU.min, op1=ALU.add)\
                        .then_inc(S["x_done"], 1)
                if l == MEAN:
                    dve.wait_ge(S["obeta_done"], b + 1)
                    v.tensor_tensor(xb, oc[:], xb, ALU.add).then_inc(S["x_done"], 1)
                if l == CHAN:
                    dve.wait_ge(S["att_done"], avg_item(l, b))
                    v.tensor_tensor(xb, att[:], xb, ALU.add).then_inc(S["x_done"], 1)
                if l == ATT3:
                    dve.wait_ge(S["att_done"], avg_item(l, b))
                    v.scalar_tensor_tensor(out=xb, in0=att[:], scalar=0.0, in1=xb, op0=ALU.max, op1=ALU.add)\
                        .then_inc(S["x_done"], 1)

            def step(a, b, m, f, half):
                other = 1 - half
                from_chan = f and f[0] == CHAN
                if b and b[0] in ATT:
                    sum_A(a)
                    max_B(b, other)
                    cent_A(a)
                    diff_F(f, other)
                    if not from_chan:
                        rden_F(f, other)
                    var_A(a)
                    diag_B(b)
                    cmp_B(b, other, 0, 1)
                    if from_chan:
                        fill(f, other)
                    cmp_B(b, other, 1, 2)
                    miss_B(b, other, 0)
                    if not from_chan:
                        att_F(f, other)
                    cmp_B(b, other, 2, 3)
                    miss_B(b, other, 1)
                    h_A(a, half)
                    shift_B(b, other)
                    pos_F(f)
                    hm_B(b, f, other)
                    cmp_B(b, other, 3, 4)
                    miss_B(b, other, 2)
                    top_B(b, other)
                    cmp_B(b, other, 4, 5)
                    rest_B(b, other)
                    cmp_B(b, other, 5, 6)
                    if not from_chan:
                        x_F(f)
                    low_B(b, other)
                    cmp_B(b, other, 6, T)
                    if from_chan:
                        rden_F(f, other)
                        att_F(f, other)
                        x_F(f)
                elif b and from_chan:
                    max_B(b, other)
                    sum_A(a)
                    cent_A(a)
                    diff_F(f, other)
                    diag_B(b)
                    fill(f, other)
                    var_A(a)
                    shift_B(b, other)
                    hm_B(b, f, other)
                    h_A(a, half)
                    top_B(b, other)
                    rest_B(b, other)
                    low_B(b, other)
                    rden_F(f, other)
                    att_F(f, other)
                    feat_A(a, half)
                    x_F(f)
                else:
                    max_B(b, other)
                    sum_A(a)
                    cent_A(a)
                    diff_F(f, other)
                    var_A(a)
                    rden_F(f, other)
                    if f and f[0] == CHAN:
                        fill(f, other)
                    diag_B(b)
                    att_F(f, other)
                    shift_B(b, other)
                    ovar_F(f)
                    if b and b[0] == MEAN:
                        rest_B(b, other)
                    pos_F(f)
                    hm_B(b, f, other)
                    h_A(a, half)
                    if b and b[0] == MEAN:
                        low_B(b, other)
                    self_B(b, f, other)
                    scale_F(f)
                    top_B(b, other)
                    beta_F(f)
                    if b and b[0] == CHAN:
                        rest_B(b, other)
                    x_F(f)
                    if b and b[0] == CHAN:
                        low_B(b, other)
                    feat_A(a, half)

            for g in range(2):
                dve.wait_ge(S["w_in"], W_IN)
                v.tensor_copy(arep[g][:], acol[g][:, 0:1].to_broadcast([D, P])).then_inc(S["arep_sb"], 1)
            for g in range(2):
                dve.wait_ge(S["wt_ps"], g + 1)
                v.tensor_copy(wtr[g][:], acc[0:D, g, 0:D]).then_inc(S["wt_sb"], 1)
            dve.wait_ge(S["const_g"], 1)
            sum_A((0, 0))
            cent_A((0, 0))
            for g in range(2):
                dve.wait_ge(S["wa_ps"], g + 1)
                for half in range(2):
                    q, o = slice(half * D, half * D + D), half * G
                    v.tensor_copy(wext[g][q, o:o + 2], acc[0:D, g, 128:130])
                    v.tensor_copy(w1rep[g][q], acc[0:D, g, 256:256 + P])
                    v.tensor_copy(wstack[g][q], wnat[g][:] if g == 0 else wtr[g][:])
                    last = v.tensor_copy(wext[g][q, o + 2:o + G], wnat[g][:] if g == 0 else wtr[g][:])
                last.then_inc(S["wa_sb"], 1)
            var_A((0, 0))
            h_A((0, 0), 0)
            sum_A((0, 1))
            cent_A((0, 1))

            def mask_part(t):
                dve.wait_ge(S[f"adj_in{t // 2}"], 16)
                v.tensor_scalar(mask[:, t], adj[:, t], 0.0, None, ALU.is_gt).then_inc(S["mask_nat"], 1)

            def maskT_part(t):
                dve.wait_ge(S["mask_tr"], t + 1)
                v.tensor_copy(maskT[:, :, t * P:(t + 1) * P], mask_bank(t)).then_inc(S["maskT_dve"], 1)

            mask_part(0)
            mask_part(1)
            max_B((0, 0), 0)
            var_A((0, 1))
            diag_B((0, 0))
            mask_part(2)
            mask_part(3)
            h_A((0, 1), 1)
            maskT_part(0)
            shift_B((0, 0), 0)
            hm_B((0, 0), None, 0)
            maskT_part(1)
            mask_part(4)
            mask_part(5)
            top_B((0, 0), 0)
            maskT_part(2)
            rest_B((0, 0), 0)
            mask_part(6)
            mask_part(7)
            maskT_part(4)
            maskT_part(5)
            low_B((0, 0), 0)
            maskT_part(6)
            dve.wait_ge(S["maskT_act"], 2)
            dve.wait_ge(S["maskT_dve"], T - 2)
            for t in range(CH):
                v.tensor_scalar(nmaskT[:, t], maskT[:, t], -1.0, None, ALU.mult).then_inc(S["nmask_dve"], 1)
            cmp_B((0, 0), 0, 0, T)
            dve.wait_ge(S["nmask_act"], T - CH)
            dve.wait_ge(S["nmask_dve"], CH)
            for j in range(SPLIT):
                miss_B((0, 0), 0, j)
            dve.wait_ge(S["rows_ps"], 1)
            v.tensor_copy(par_rows[:], acc[:, CH - 2, 0:NR * D + 2]).then_inc(S["rows_sb"], 1)
            dve.wait_ge(S["rows_sb"], 1)
            v.tensor_scalar(k0[:], par_rows[:, NR * D:NR * D + 1], 0.7071067811865476, None, ALU.mult)
            v.tensor_copy(b0[:], par_rows[:, NR * D + 1:NR * D + 2])
            dve.wait_ge(S["deg_ps"], 1)
            v.tensor_copy(deg[:], acc[:, CH - 1, DEG:DEG + T]).then_inc(S["deg_sb"], 1)
            dve.wait_ge(S["deg_sb"], 1)
            v.tensor_scalar(lone[:], deg[:], 0.0, None, ALU.is_equal)
            v.tensor_scalar(some[:], deg[:], 0.0, None, ALU.is_gt)
            v.tensor_scalar(deg1[:], deg[:], 1.0, None, ALU.max).then_inc(S["deg1_sb"], 1)
            dve.wait_ge(S["deg1_sb"], 1)
            v.reciprocal(rdeg[:], deg1[:])
            v.tensor_tensor(base[:], along(par_row(B_NEIGH)), spread(some[:], D), ALU.mult).then_inc(S["base_sb"], 1)
            dve.wait_ge(S["base_sb"], 1)
            v.tensor_tensor(base[:], base[:], along(par_row(B_SELF)), ALU.add).then_inc(S["base2_sb"], 1)
            dve.wait_ge(S["base2_sb"], 1)
            run(dve, step)

        @block.scalar
        def _(act):
            s = nc.scalar

            def sq_A(a):
                if a:
                    act.wait_ge(S["ln_cent"], item(*a))
                    s.activation(sq[:], cent[:], ACT.Square, scale=float(D) ** -0.5).then_inc(S["ln_sq"], 1)

            def hT_A(a, par):
                if a and a[0] != CHAN:
                    act.wait_ge(S["tr_done"], tr_item(*a))
                    s.activation(hT[:].rearrange("p k n -> p (k n)"), tp[:, 0], ACT.Copy,
                                 accum_out=hsum[:, par:par + 1]).then_inc(S["hT_done"], 1)

            def hp_A(a, par):
                if not a or a[0] == CHAN:
                    return
                act.wait_ge(S["pj_done"], tr_item(*a))
                g, o = (2 * D, hc[:, par]) if a[0] == MEAN else (G, hp[:, par, :, 0:G])
                s.activation(o.rearrange("p (k t) g -> p k t g", k=2),
                             pj[:, :, 0:T // 2 * g].rearrange("p k (t g) -> p k t g", g=g), ACT.Copy)\
                    .then_inc(S["hc_done" if a[0] == MEAN else "hp_done"], 1)

            def s1_A(a):
                if a and a[0] in ATT:
                    if not very_first(a):
                        act.wait_ge(S["reach_done"], T * (att_item(*a) - 1))
                    act.wait_ge(S["s1_done"], att_item(*a))
                    s.activation(s1bc[:].rearrange("p (t k n) -> p k t n", k=2, n=P),
                                 tp[:].rearrange("p k (t n) -> p k t n", n=P), ACT.Copy).then_inc(S["s1bc_done"], 1)

            def soft_A(a, par):
                if not a or a[0] != CHAN:
                    return
                n = a[1] + 1
                act.wait_ge(S["h_done"], item(*a))
                s.activation(ab[:], h[:, par], ACT.Abs, scale=k0[:], bias=b0[:]).then_inc(S["ab_done"], 1)
                s.activation(rl, h[:, par], ACT.Relu, scale=k0[:], bias=b0[:])
                act.wait_ge(S["ab_done"], n)
                s.activation(sp, ab[:], ACT.Exp, scale=-1.0).then_inc(S["e1_done"], 1)
                act.wait_ge(S["e1_done"], n)
                s.activation(sp, sp, ACT.Ln, bias=1.0).then_inc(S["ln1_done"], 1)

            def top_B(b, par):
                if b and b[0] == MEAN:
                    act.wait_ge(S["hc_done"], b[1] + 1)
                    s.activation(top[:, par, :, 0:D], hc[:, par, :, D:2 * D], ACT.Copy).then_inc(S["topcopy_done"], 1)

            def ex_B(b, par):
                if b and b[0] in ATT:
                    act.wait_ge(S["pre_done"], att_item(*b))
                    s.activation(ex[:, par], pre[:], ACT.Exp).then_inc(S["ex_done"], 1)

            def reach_B(b, par, j0, j1):
                if not b or b[0] not in ATT:
                    return
                n = att_item(*b)
                if j0 == 0:
                    act.wait_ge(S["s2big_done"], n)
                    act.wait_ge(S["s1bc_done"], n)
                for j in range(j0, j1):
                    s.activation(reach[:, j], s1bc[:], ACT.Relu, scale=BIG, bias=s2big[:, par, j:j + 1])\
                        .then_inc(S["reach_done"], 1)

            def ee_B(b, par):
                if b and b[0] == CHAN:
                    act.wait_ge(S["scm_done"], b[1] + 1)
                    s.activation(ee[:], sc[:, par], ACT.Exp, scale=0.5).then_inc(S["ee_done"], 1)
                    act.wait_ge(S["ee_done"], b[1] + 1)
                    s.activation(top[:, par, :, D:2 * D], ee[:], ACT.Square, scale=BIG_E ** 0.5).then_inc(S["chE_done"], 1)

            def evac_M(m, par, c):
                if not m:
                    return
                l = m[0]
                if c == 0 and (l == CHAN or l == ATT3 and isinstance(m[1], int) and m[1] < 2):
                    act.wait_ge(S["x_done"], item(*m) - 2)
                act.wait_ge(S["main_done"], CH * (item(*m) - 1) + c + 1)
                for t in range(2 * c, 2 * c + 2):
                    o = t % 2 * VQ
                    if l in ATT:
                        s.activation(num[:, par, t, 0:V], acc[:, c, o:o + V], ACT.Copy, scale=ex[:, par, 2, t:t + 1])
                        last = s.activation(num[:, par, t, V:VQ], acc[:, c, o + V:o + VQ], ACT.Copy,
                                            scale=ex[:, par, 3, t:t + 1])
                    if l == MEAN:
                        last = s.activation(num[:, par, t, 0:D], acc[:, c, o:o + D], ACT.Copy, scale=rdeg[:, t:t + 1])
                    if l == CHAN:
                        s.activation(num[:, par, t, 0:D], acc[:, c, o:o + D], ACT.Copy)
                        last = s.activation(num[:, par, t, D:2 * D], acc[:, c, o + D:o + 2 * D], ACT.Identity,
                                            bias=lone[:, t:t + 1])
                last.then_inc(S["acc_free"], 1)

            def relu_F(f):
                if f and f[0] == MEAN:
                    act.wait_ge(S["conv_done"], f[1] + 1)
                    s.activation(sr[:], conv[:], ACT.Relu).then_inc(S["conv_relu_done"], 1)

            def sq_F(f):
                if f and f[0] == MEAN:
                    act.wait_ge(S["ocent_done"], f[1] + 1)
                    s.activation(osq[:], oc[:], ACT.Square, scale=float(D) ** -0.5).then_inc(S["osq_done"], 1)

            def elu_F(f):
                if f and f[0] == ATT0:
                    act.wait_ge(S["att_done"], avg_item(*f))
                    s.activation(en[:], att[:], ACT.Exp).then_inc(S["en_done"], 1)
                    act.wait_ge(S["en_done"], f[1] + 1)
                    s.activation(em1[:], en[:], ACT.Identity, bias=mone[:]).then_inc(S["em1_done"], 1)

            def step(a, b, m, f, half):
                other = 1 - half
                chan = m and b and m[0] == b[0] == CHAN
                sq_A(a)
                if f and f[0] in ATT:
                    evac_M(f, other, 3)
                reach_B(b, other, 0, 1)
                relu_F(f)
                top_B(b, other)
                reach_B(b, other, 1, 3)
                evac_M(m, half, 0)
                sq_F(f)
                ee_B(b, other)
                reach_B(b, other, 3, 4)
                ex_B(b, other)
                elu_F(f)
                if not chan:
                    evac_M(m, half, 1)
                if m and m[0] == MEAN:
                    evac_M(m, half, 2)
                    evac_M(m, half, 3)
                reach_B(b, other, 4, 5)
                hT_A(a, half)
                reach_B(b, other, 5, 7)
                if m and m[0] != MEAN and not chan:
                    evac_M(m, half, 2)
                reach_B(b, other, 7, T)
                hp_A(a, half)
                s1_A(a)
                soft_A(a, half)
                if chan:
                    evac_M(m, half, 1)
                    evac_M(m, half, 2)
                if m and m[0] == CHAN:
                    evac_M(m, half, 3)

            def maskT_part(t):
                act.wait_ge(S["mask_tr"], t + 1)
                s.activation(maskT[:, :, t * P:(t + 1) * P], mask_bank(t), ACT.Copy).then_inc(S["maskT_act"], 1)

            av = adj_in.rearrange("(p t) n -> p t n", t=T)
            for g, (w, a) in enumerate(((w_in["L0_gnn_W"], w_in["L0_gnn_a"]), (w_in["L3_gnn_W"], w_in["L3_gnn_a"]))):
                act.dma_start(wnat[g][:], w).then_inc(S["w_in"], 16)
                for c in range(2):
                    act.dma_start(acol[g][:, c:c + 1], a[c * D:(c + 1) * D, :]).then_inc(S["w_in"], 16)
            for t in range(0, T, 2):
                act.dma_start(adj[:, t:t + 2], av[:, t:t + 2]).then_inc(S[f"adj_in{t // 2}"], 16)
            sq_A((0, 0))
            hT_A((0, 0), 0)
            hp_A((0, 0), 0)
            sq_A((0, 1))
            s1_A((0, 0))
            reach_B((0, 0), 0, 0, 2)
            hT_A((0, 1), 1)
            reach_B((0, 0), 0, 2, 4)
            ex_B((0, 0), 0)
            maskT_part(3)
            hp_A((0, 1), 1)
            reach_B((0, 0), 0, 4, T)
            maskT_part(7)
            act.wait_ge(S["maskT_act"], 2)
            act.wait_ge(S["maskT_dve"], T - 2)
            for t in range(CH, T):
                s.activation(nmaskT[:, t], maskT[:, t], ACT.Copy, scale=-1.0).then_inc(S["nmask_act"], 1)
            s1_A((0, 1))
            run(act, step)

        @block.tensor
        def _(pe):
            mm = nc.tensor.matmul

            def tr_A(a, par):
                if not a or a[0] == CHAN:
                    return
                if not very_first(a):
                    pe.wait_ge(S["s1bc_done"], B if a[0] == MEAN else att_item(*a) - 1)
                pe.wait_ge(S["h_done"], item(*a))
                for t in range(T // 2):
                    last = nc.tensor.transpose(tp[:, 0, t * P:(t + 1) * P],
                                               h[:, par, 2 * t:2 * t + 2].rearrange("p t d -> p (t d)"), ident[:])
                last.then_inc(S["tr_done"], 1)

            def proj_A(a, b):
                if not a or a[0] == CHAN:
                    return
                if b and b[0] != MEAN:
                    pe.wait_ge(S["hm_done"], avg_item(*b))
                if b and b[0] == MEAN:
                    pe.wait_ge(S["hc_done"], b[1] + 1)
                w = wconv if a[0] == MEAN else wext[a[0] // 3]
                g = 4 * D if a[0] == MEAN else 2 * G
                pe.wait_ge(S["hT_done"], tr_item(*a))
                for t in range(T // 2):
                    o = t % 2 * g
                    last = mm(pj[:, t // 2, o:o + g], hT[:, t], w[:, 0:g], start=True, stop=True)
                last.then_inc(S["pj_done"], 1)

            def s1_A(a):
                if a and a[0] in ATT:
                    for k in range(2):
                        q = slice(k * D, k * D + D)
                        last = mm(tp[:, k], w1rep[a[0] // 3][q], hT[q].rearrange("p t n -> p (t n)"), start=True, stop=True)
                    last.then_inc(S["s1_done"], 1)

            def mxt_B(b, par):
                if not b or b[0] == MEAN:
                    return
                pe.wait_ge(S["smx_done"], avg_item(*b))
                last = nc.tensor.transpose(pj[:, 1, 0:P], smx[:], ident[:])
                if b[0] == CHAN:
                    for t in range(T):
                        last = mm(pj[0:D, 0, 0:1], feat[:, par, t], avg[:], start=(t == 0), stop=(t == T - 1))
                last.then_inc(S["mxt_done"], 1)

            def mbc_B(b, par):
                if not b or b[0] == MEAN:
                    return
                if b[0] == CHAN:
                    pe.wait_ge(S["diag_done"], b[1] + 1)
                    last = mm(pj[:, 1, MEANS:MEANS + 2 * D], ones[0:D], diag[:], start=True, stop=True)
                else:
                    pe.wait_ge(S["mcol_done"], avg_item(*b))
                    mm(pj[:, 1, MAXIMA:MAXIMA + 1], ones[0:1], mcol[0:1], start=True, stop=True)
                    last = mm(pj[:, 1, MEANS:MEANS + D], hsum[:, par:par + 1].to_broadcast([P, P]), wstack[b[0] // 3][:],
                              start=True, stop=True)
                last.then_inc(S["mbc_done"], 1)

            def main_M(m, par, i):
                if not m:
                    return
                l = m[0]
                c, w, o = i // 2, width[l], i % 2 * VQ
                if i == 0:
                    pe.wait_ge(S["low_done"], item(*m))
                if i % 2 == 0 and not very_first(m):
                    pe.wait_ge(S["acc_free"], freed(*m, c + 1 - CH))
                if i == T - 4 and very_first(m):
                    pe.wait_ge(S["rows_sb"], 1)
                if i == T - 2 and very_first(m):
                    pe.wait_ge(S["deg_sb"], 1)
                cuts = (upper(top[:, par]), upper(rest[:, par]), low[:, par])
                rowt = slice(i * P, (i + 1) * P)
                if l in ATT:
                    for j in [*range(SPLIT, T), *range(SPLIT)]:
                        if i == 0:
                            pe.wait_ge(S["c_done"], T * (att_item(*m) - 1) + j + 1)
                        wj = V if j < SPLIT else VQ
                        for s_ in range(3):
                            mm(acc[:, c, o:o + wj], C[:, par, j, rowt], cuts[s_][:, j, 0:wj],
                               start=(j == SPLIT and s_ == 0), stop=False)
                    if i == 0:
                        pe.wait_ge(S["miss_done"], SPLIT * att_item(*m))
                        if very_first(m):
                            pe.wait_ge(S["nmask_dve"], CH)
                            pe.wait_ge(S["nmask_act"], T - CH)
                    for j in range(T):
                        lhs = miss_tile(par, j)[:, rowt] if j < SPLIT else nmaskT[:, j, rowt]
                        for s_ in range(3):
                            last = mm(acc[:, c, o + V:o + VQ], lhs, cuts[s_][:, j, V:VQ],
                                      start=False, stop=(j == T - 1 and s_ == 2))
                else:
                    for j in range(T):
                        for s_ in range(3):
                            last = mm(acc[:, c, o:o + w], maskT[:, j, rowt], cuts[s_][:, j, 0:w],
                                      start=(j == 0 and s_ == 0), stop=(j == T - 1 and s_ == 2))
                if i % 2 == 1:
                    last.then_inc(S["main_done"], 1)

            def step(a, b, m, f, half):
                other = 1 - half
                wide = m and m[0] in ATT
                within = wide or a and a[0] in ATT
                main_M(m, half, 0)
                main_M(m, half, 1)
                mxt_B(b, other)
                if not wide:
                    mbc_B(b, other)
                main_M(m, half, 2)
                if wide:
                    mbc_B(b, other)
                main_M(m, half, 3)
                main_M(m, half, 4)
                if within:
                    tr_A(a, half)
                main_M(m, half, 5)
                if within and not wide:
                    proj_A(a, b)
                main_M(m, half, 6)
                if wide:
                    proj_A(a, b)
                elif within:
                    s1_A(a)
                main_M(m, half, 7)
                if wide:
                    s1_A(a)
                elif not within:
                    tr_A(a, half)
                    proj_A(a, b)

            pe.wait_ge(S["identb_g"], 1)
            pe.wait_ge(S["w_in"], W_IN)
            for g in range(2):
                nc.tensor.transpose(acc[0:D, g, 0:D], wnat[g][:], ident[0:D, 0:D]).then_inc(S["wt_ps"], 1)
            pe.wait_ge(S["arep_sb"], 2)
            for g in range(2):
                pe.wait_ge(S["wt_sb"], g + 1)
                w = wtr[g] if g == 0 else wnat[g]
                mm(acc[0:D, g, 128:130], w[:], acol[g][:], start=True, stop=True)
                mm(acc[0:D, g, 256:256 + P], w[:], arep[g][:], start=True, stop=True).then_inc(S["wa_ps"], 1)
            pe.wait_ge(S["wa_sb"], 2)

            def mask_tr(t):
                pe.wait_ge(S["mask_nat"], t + 1)
                if t >= CH:
                    if t == T - 1:
                        pe.wait_ge(S["maskT_act"], 1)
                    else:
                        pe.wait_ge(S["maskT_dve"], t - CH + 1)
                for j in range(T):
                    last = nc.tensor.transpose(acc[:, t % CH].bitcast(BF16)[:, j * P:(j + 1) * P],
                                               mask[:, t].rearrange("p (q j) -> p j q", j=T)[:, j], identb[:])
                last.then_inc(S["mask_tr"], 1)

            tr_A((0, 0), 0)
            proj_A((0, 0), None)
            s1_A((0, 0))
            mxt_B((0, 0), 0)
            mask_tr(0)
            mask_tr(1)
            mbc_B((0, 0), 0)
            mask_tr(2)
            mask_tr(3)
            tr_A((0, 1), 1)
            mask_tr(4)
            proj_A((0, 1), (0, 0))
            mask_tr(5)
            s1_A((0, 1))
            mask_tr(6)
            mask_tr(7)
            pe.wait_ge(S["maskT_act"], 2)
            pe.wait_ge(S["maskT_dve"], T - 2)
            for i in range(T):
                for j in range(T):
                    last = mm(acc[:, CH - 1, DEG + i:DEG + i + 1], maskT[:, j, i * P:(i + 1) * P], onesb[:],
                              start=(j == 0), stop=(j == T - 1))
            last.then_inc(S["deg_ps"], 1)
            pe.wait_ge(S["row_in"], ROW_IN)
            mm(acc[:, CH - 2, 0:NR * D + 2], ones[0:1, :], rows[:], start=True, stop=True).then_inc(S["rows_ps"], 1)
            run(pe, step)


_WEIGHTS = ['L0_gnn_W', 'L0_gnn_a', 'L1_gnn_W_self', 'L1_gnn_b_self', 'L1_gnn_W_neigh', 'L1_gnn_b_neigh',
            'L1_gnn_ln_gamma', 'L1_gnn_ln_beta', 'L2_gnn_w0', 'L2_gnn_b0', 'L2_gnn_wa', 'L2_gnn_ba',
            'L3_gnn_W', 'L3_gnn_a']


def kernel(**inputs):
    import numpy as _np
    import concourse.bacc as _bacc
    from concourse import mybir as _mybir
    from concourse.bass_utils import run_bass_kernel_spmd as _run

    nc = _bacc.Bacc("TRN2", target_bir_lowering=False, num_devices=1)
    arrays, aps = {}, {}
    for name in ['x', 'adj'] + _WEIGHTS:
        a = _np.ascontiguousarray(inputs[name])
        arrays[f"in_{name}"] = a
        aps[name] = nc.dram_tensor(f"in_{name}", a.shape, _mybir.dt.from_np(a.dtype), kind="ExternalInput").ap()
    o = nc.dram_tensor("out_x", inputs['x'].shape, _mybir.dt.float32, kind="ExternalOutput").ap()
    build(nc, aps['x'], aps['adj'], {n: aps[n] for n in _WEIGHTS}, o)
    r = _run(nc, [arrays], core_ids=[0])
    return r.results[0]["out_x"]
```
